# Optimizing a Trainium2 kernel written in Bass

```python
import numpy as np
import jax
import jax.numpy as jnp

def _softmax(x, axis=-1):
    return jax.nn.softmax(x, axis=axis)

def _gelu(x):
    return jax.nn.gelu(x, approximate=True)

def _silu(x):
    return jax.nn.silu(x)

def _sigmoid(x):
    return jax.nn.sigmoid(x)

def _layernorm(x, axis=-1, eps=1e-05):
    m = jnp.mean(x, axis=axis, keepdims=True)
    v = jnp.var(x, axis=axis, keepdims=True)
    return (x - m) / jnp.sqrt(v + eps)

def _scatter_add(tgt, idx, src, axis=0):
    return tgt.at[idx].add(src)

def _segment_sum(src, seg, n):
    return jax.ops.segment_sum(src, seg, n)
kernel_name = 'mk_hybrid_d1_jaxref_r8_90fca9'

def setup_inputs(seed: int=0):
    np.random.seed(seed)
    _w = jnp.asarray

    def _L0_attn_a_setup():
        import jax, jax.numpy as jnp
        import numpy as np
        D_MODEL = 128
        OMEGA_DIM = 64
        VQ_CODES = 32
        VQ_DIM = 64
        N_PARAMS = OMEGA_DIM * (OMEGA_DIM - 1) // 2
        TRIU_R, TRIU_C = np.triu_indices(OMEGA_DIM, k=1)
        RMS_EPS = 1e-06
        NORM_EPS = 1e-12

        def _normalize(v):
            n = jnp.linalg.norm(v, axis=-1, keepdims=True)
            return v / jnp.maximum(n, NORM_EPS)

        def _rmsnorm(x, w):
            ms = jnp.mean(x * x, axis=-1, keepdims=True)
            return x * jax.lax.rsqrt(ms + RMS_EPS) * w
        key = jax.random.key(seed)
        ks = jax.random.split(key, 12)
        B, L = (16, 512)
        s = 0.02
        return {'x': jax.random.normal(ks[0], (B, L, D_MODEL), jnp.float32), 'omega_proj_w': jax.random.normal(ks[1], (N_PARAMS, D_MODEL), jnp.float32) * s, 'omega_proj_b': jnp.zeros((N_PARAMS,), jnp.float32), 'omega_out_w': jax.random.normal(ks[2], (D_MODEL, OMEGA_DIM), jnp.float32) * s, 'omega_out_b': jnp.zeros((D_MODEL,), jnp.float32), 'vq_proj_in_w': jax.random.normal(ks[3], (VQ_DIM, D_MODEL), jnp.float32) * s, 'vq_proj_in_b': jnp.zeros((VQ_DIM,), jnp.float32), 'vq_proj_out_w': jax.random.normal(ks[4], (D_MODEL, VQ_DIM), jnp.float32) * s, 'vq_proj_out_b': jnp.zeros((D_MODEL,), jnp.float32), 'codebook': jax.random.normal(ks[5], (VQ_CODES, VQ_DIM), jnp.float32), 'omega_mix': jnp.float32(0.1), 'vq_mix': jnp.float32(0.05), 'norm_w': jnp.ones((D_MODEL,), jnp.float32)}
    _L0_attn_a_in = _L0_attn_a_setup()

    def _L0_attn_b_setup():
        import jax, jax.numpy as jnp
        import numpy as np
        E = 128
        H = 16
        D = E // H

        def _mha(x, Wq, bq, Wk, bk, Wv, bv, Wo, bo):
            q = jnp.einsum('bse,hde->bhsd', x, Wq) + bq[None, :, None, :]
            k = jnp.einsum('bse,hde->bhsd', x, Wk) + bk[None, :, None, :]
            v = jnp.einsum('bse,hde->bhsd', x, Wv) + bv[None, :, None, :]
            scores = jnp.einsum('bhsd,bhtd->bhst', q, k) / jnp.sqrt(jnp.asarray(D, x.dtype))
            w = jax.nn.softmax(scores, axis=-1)
            o = jnp.einsum('bhst,bhtd->bhsd', w, v)
            B, _, S, _ = o.shape
            o = jnp.transpose(o, (0, 2, 1, 3)).reshape(B, S, H * D)
            return o @ Wo.T + bo
        key = jax.random.key(seed)
        ks = jax.random.split(key, 9)
        s = 0.02
        return {'hidden_state': jax.random.normal(ks[0], (4, 128, E), jnp.float32), 'Wq': jax.random.normal(ks[1], (H, D, E), jnp.float32) * s, 'bq': jax.random.normal(ks[2], (H, D), jnp.float32) * s, 'Wk': jax.random.normal(ks[3], (H, D, E), jnp.float32) * s, 'bk': jax.random.normal(ks[4], (H, D), jnp.float32) * s, 'Wv': jax.random.normal(ks[5], (H, D, E), jnp.float32) * s, 'bv': jax.random.normal(ks[6], (H, D), jnp.float32) * s, 'Wo': jax.random.normal(ks[7], (E, E), jnp.float32) * s, 'bo': jax.random.normal(ks[8], (E,), jnp.float32) * s}
    _L0_attn_b_in = _L0_attn_b_setup()

    def _L0_ffn_setup():
        import jax, jax.numpy as jnp
        import numpy as np
        B, T, D, E, H, K = (4, 256, 128, 8, 256, 2)
        key = jax.random.key(seed)
        k0, k1, k2, k3 = jax.random.split(key, 4)
        x = jax.random.normal(k0, (B, T, D), dtype=jnp.float32)
        router_w = jax.random.normal(k1, (E, D), dtype=jnp.float32) * D ** (-0.5)
        w1 = jax.random.normal(k2, (E, D, H), dtype=jnp.float32) * D ** (-0.5)
        w2 = jax.random.normal(k3, (E, H, D), dtype=jnp.float32) * H ** (-0.5)
        return {'x': x, 'router_w': router_w, 'w1': w1, 'w2': w2}
    _L0_ffn_in = _L0_ffn_setup()
    _d = {'L0_attn_a_x': _L0_attn_a_in['x'], 'L0_attn_a_omega_proj_w': _L0_attn_a_in['omega_proj_w'], 'L0_attn_a_omega_proj_b': _L0_attn_a_in['omega_proj_b'], 'L0_attn_a_omega_out_w': _L0_attn_a_in['omega_out_w'], 'L0_attn_a_omega_out_b': _L0_attn_a_in['omega_out_b'], 'L0_attn_a_vq_proj_in_w': _L0_attn_a_in['vq_proj_in_w'], 'L0_attn_a_vq_proj_in_b': _L0_attn_a_in['vq_proj_in_b'], 'L0_attn_a_vq_proj_out_w': _L0_attn_a_in['vq_proj_out_w'], 'L0_attn_a_vq_proj_out_b': _L0_attn_a_in['vq_proj_out_b'], 'L0_attn_a_codebook': _L0_attn_a_in['codebook'], 'L0_attn_a_omega_mix': _L0_attn_a_in['omega_mix'], 'L0_attn_a_vq_mix': _L0_attn_a_in['vq_mix'], 'L0_attn_a_norm_w': _L0_attn_a_in['norm_w'], 'L0_attn_b_Wq': _L0_attn_b_in['Wq'], 'L0_attn_b_bq': _L0_attn_b_in['bq'], 'L0_attn_b_Wk': _L0_attn_b_in['Wk'], 'L0_attn_b_bk': _L0_attn_b_in['bk'], 'L0_attn_b_Wv': _L0_attn_b_in['Wv'], 'L0_attn_b_bv': _L0_attn_b_in['bv'], 'L0_attn_b_Wo': _L0_attn_b_in['Wo'], 'L0_attn_b_bo': _L0_attn_b_in['bo'], 'L0_ffn_router_w': _L0_ffn_in['router_w'], 'L0_ffn_w1': _L0_ffn_in['w1'], 'L0_ffn_w2': _L0_ffn_in['w2']}
    _x0 = _d['L0_attn_a_x']
    _d['L0_attn_a_x'] = jax.random.normal(jax.random.fold_in(jax.random.key(seed), 1), (4, 1024, 128), dtype=_x0.dtype)
    del _x0
    return _d

def reference(L0_attn_a_x, L0_attn_a_omega_proj_w, L0_attn_a_omega_proj_b, L0_attn_a_omega_out_w, L0_attn_a_omega_out_b, L0_attn_a_vq_proj_in_w, L0_attn_a_vq_proj_in_b, L0_attn_a_vq_proj_out_w, L0_attn_a_vq_proj_out_b, L0_attn_a_codebook, L0_attn_a_omega_mix, L0_attn_a_vq_mix, L0_attn_a_norm_w, L0_attn_b_Wq, L0_attn_b_bq, L0_attn_b_Wk, L0_attn_b_bk, L0_attn_b_Wv, L0_attn_b_bv, L0_attn_b_Wo, L0_attn_b_bo, L0_ffn_router_w, L0_ffn_w1, L0_ffn_w2):

    def _L0_attn_a_ref(x, omega_proj_w, omega_proj_b, omega_out_w, omega_out_b, vq_proj_in_w, vq_proj_in_b, vq_proj_out_w, vq_proj_out_b, codebook, omega_mix, vq_mix, norm_w):
        import jax, jax.numpy as jnp
        import numpy as np
        D_MODEL = 128
        OMEGA_DIM = 64
        VQ_CODES = 32
        VQ_DIM = 64
        N_PARAMS = OMEGA_DIM * (OMEGA_DIM - 1) // 2
        TRIU_R, TRIU_C = np.triu_indices(OMEGA_DIM, k=1)
        RMS_EPS = 1e-06
        NORM_EPS = 1e-12

        def _normalize(v):
            n = jnp.linalg.norm(v, axis=-1, keepdims=True)
            return v / jnp.maximum(n, NORM_EPS)

        def _rmsnorm(x, w):
            ms = jnp.mean(x * x, axis=-1, keepdims=True)
            return x * jax.lax.rsqrt(ms + RMS_EPS) * w
        B = x.shape[0]
        residual = x
        h_mean = jnp.mean(x, axis=1)
        params = h_mean @ omega_proj_w.T + omega_proj_b
        omega = jnp.zeros((B, OMEGA_DIM, OMEGA_DIM), x.dtype).at[:, TRIU_R, TRIU_C].set(params)
        omega = omega - jnp.swapaxes(omega, -1, -2)
        I = jnp.eye(OMEGA_DIM, dtype=x.dtype)
        omega2 = jnp.einsum('bij,bjk->bik', omega, omega)
        omega3 = jnp.einsum('bij,bjk->bik', omega2, omega)
        G = I + omega + 0.5 * omega2 + 1.0 / 6.0 * omega3
        x_head = x[:, :, :OMEGA_DIM]
        x_rotated = jnp.einsum('bld,bde->ble', x_head, G)
        lie_out = x_rotated @ omega_out_w.T + omega_out_b
        vq_input = h_mean @ vq_proj_in_w.T + vq_proj_in_b
        scores = _normalize(vq_input) @ _normalize(codebook).T
        vq_idx = jnp.argmax(scores, axis=-1)
        vq_code = codebook[vq_idx]
        vq_out = vq_input + jax.lax.stop_gradient(vq_code - vq_input)
        vq_contribution = (vq_out @ vq_proj_out_w.T + vq_proj_out_b)[:, None, :]
        out = residual + omega_mix * lie_out + vq_mix * vq_contribution
        return _rmsnorm(out, norm_w)

    def _L0_attn_b_ref(hidden_state, Wq, bq, Wk, bk, Wv, bv, Wo, bo):
        import jax, jax.numpy as jnp
        import numpy as np
        E = 128
        H = 16
        D = E // H

        def _mha(x, Wq, bq, Wk, bk, Wv, bv, Wo, bo):
            q = jnp.einsum('bse,hde->bhsd', x, Wq) + bq[None, :, None, :]
            k = jnp.einsum('bse,hde->bhsd', x, Wk) + bk[None, :, None, :]
            v = jnp.einsum('bse,hde->bhsd', x, Wv) + bv[None, :, None, :]
            scores = jnp.einsum('bhsd,bhtd->bhst', q, k) / jnp.sqrt(jnp.asarray(D, x.dtype))
            w = jax.nn.softmax(scores, axis=-1)
            o = jnp.einsum('bhst,bhtd->bhsd', w, v)
            B, _, S, _ = o.shape
            o = jnp.transpose(o, (0, 2, 1, 3)).reshape(B, S, H * D)
            return o @ Wo.T + bo
        return _mha(hidden_state, Wq, bq, Wk, bk, Wv, bv, Wo, bo)

    def _L0_ffn_ref(x, router_w, w1, w2):
        import jax, jax.numpy as jnp
        import numpy as np
        B, T, D, E, H, K = (4, 256, 128, 8, 256, 2)
        Bb, Tt, Dd = x.shape
        N = Bb * Tt
        logits = jnp.einsum('btd,ed->bte', x, router_w)
        top_vals, top_idx = jax.lax.top_k(logits, K)
        top_w = jax.nn.softmax(top_vals, axis=-1)
        xf = x.reshape(N, Dd)
        h = jnp.einsum('nd,edh->enh', xf, w1)
        h = jnp.square(jax.nn.relu(h))
        y = jnp.einsum('enh,ehd->end', h, w2)
        idx_f = top_idx.reshape(N, K)
        w_f = top_w.reshape(N, K)
        y_sel = y[idx_f, jnp.arange(N)[:, None]]
        out = jnp.einsum('nk,nkd->nd', w_f, y_sel)
        return out.reshape(Bb, Tt, Dd)
    x = L0_attn_a_x
    x = x + _L0_attn_a_ref(_layernorm(x, axis=-1), L0_attn_a_omega_proj_w, L0_attn_a_omega_proj_b, L0_attn_a_omega_out_w, L0_attn_a_omega_out_b, L0_attn_a_vq_proj_in_w, L0_attn_a_vq_proj_in_b, L0_attn_a_vq_proj_out_w, L0_attn_a_vq_proj_out_b, L0_attn_a_codebook, L0_attn_a_omega_mix, L0_attn_a_vq_mix, L0_attn_a_norm_w)
    x = x + _L0_ffn_ref(_layernorm(x, axis=-1), L0_ffn_router_w, L0_ffn_w1, L0_ffn_w2)
    x = x + _L0_attn_b_ref(_layernorm(x, axis=-1), L0_attn_b_Wq, L0_attn_b_bq, L0_attn_b_Wk, L0_attn_b_bk, L0_attn_b_Wv, L0_attn_b_bv, L0_attn_b_Wo, L0_attn_b_bo)
    x = x + _L0_ffn_ref(_layernorm(x, axis=-1), L0_ffn_router_w, L0_ffn_w1, L0_ffn_w2)
    return x

_drawn_inputs = setup_inputs


def setup_inputs(seed=0):
    import zlib

    import numpy as np

    out = dict(_drawn_inputs(seed))
    spreads = {'L0_attn_a_omega_proj_b': (0.0, 0.1),
     'L0_attn_a_omega_out_b': (0.0, 0.287),
     'L0_attn_a_vq_proj_in_b': (0.0, 0.1),
     'L0_attn_a_vq_proj_out_b': (0.0, 0.341),
     'L0_attn_a_norm_w': (1.0, 0.2)}
    factors = {'L0_attn_a_omega_proj_w': 6.003,
     'L0_attn_a_vq_proj_in_w': 8.0,
     'L0_attn_b_Wq': 8.0,
     'L0_attn_b_bq': 8.0,
     'L0_attn_b_Wk': 8.0,
     'L0_attn_b_bk': 8.0,
     'L0_attn_b_Wv': 5.589,
     'L0_attn_b_bv': 5.163,
     'L0_attn_b_Wo': 4.748}
    for name, (base, spread) in spreads.items():
        noise = np.random.default_rng([zlib.crc32(name.encode()), seed]).standard_normal(out[name].shape)
        drawn = base * np.exp(spread * noise) if base else spread * noise
        out[name] = jnp.asarray(drawn.astype(out[name].dtype))
    for name, factor in factors.items():
        out[name] = (out[name] * factor).astype(out[name].dtype)
    return out
```

```python
from contextlib import ExitStack

import concourse.bass as bass
from concourse import mybir

ALU = mybir.AluOpType
ACT = mybir.ActivationFunctionType
AX = mybir.AxisListType
F32 = mybir.dt.float32
F32R = mybir.dt.float32r
I32 = mybir.dt.int32
U32 = mybir.dt.uint32

P = 128
B, L, D = 4, 1024, 128
TPB = L // P
BLK = 512
NBLK = B * L // BLK
TPK = BLK // P
OD = 64
VD, VC = 64, 32
E, HID = 8, 256
CH = HID // P
H, DH = 16, 8
HG = 4
NG = H // HG
RB = 32
STEPS = 2 * TPB
BSTEPS = NG * STEPS
LN_EPS, RMS_EPS, NORM_EPS = 1e-5, 1e-6, 1e-12
RSQRT_MAGIC = 1597463007.0
OMEGA_HALF = OD * OD // 2

C_ID, C_NMQ, C_NMK, C_IOTA, C_ONE, C_END = 0, 128, 129, 130, 162, 163


def ds(start, n):
    return bass.ds(start, n)


class Chain:

    def __init__(self, eng, sem):
        self.eng, self.sem, self.n, self.base = eng, sem, 0, 0

    def __call__(self, ins):
        self.n += 1
        ins.then_inc(self.sem, 1)
        self.eng.wait_ge(self.sem, self.base + self.n)

    def enter(self, rounds_done, per_round):
        self.base, self.n0 = rounds_done * per_round, self.n

    def leave(self, rounds, per_round):
        assert self.n - self.n0 == per_round, (self.n - self.n0, per_round)
        self.base, self.n = 0, self.n0 + rounds * per_round


FFN_CHAIN = 23
ATT_CHAIN = 44


def hybrid_layer(nc, a, out):
    ctx = ExitStack()
    with ctx:
        def sb(name, shape, dt=F32):
            return ctx.enter_context(nc.sbuf_tensor(name, shape, dt))

        def ps(name, shape, dt=F32):
            return ctx.enter_context(nc.psum_tensor(name, shape, dt))

        def sem(name):
            return ctx.enter_context(nc.semaphore(name))

        x = sb("x", [P, B * TPB * D])
        hTh = sb("hTh", [P, 4 * BLK], F32R)
        hTl = sb("hTl", [P, 4 * BLK], F32R)
        w1h = sb("w1h", [P, E * HID], F32R)
        w1l = sb("w1l", [P, E * HID], F32R)
        w2s = sb("w2s", [P, E * CH, D])
        Km = sb("Km", [P, NG, HG, L], F32R)
        Q = sb("Q", [P, NG, L], F32R)
        PB = sb("PB", [P, 2, HG, BLK])
        SC = sb("SC", [P, 4096])
        VH = sb("VH", [P, 2048])
        Vg = sb("Vg", [P, 2, TPB, HG, RB])
        Kst = sb("Kst", [P, BLK], F32R)
        tr = sb("tr", [P, BLK], F32R)
        wqh = sb("wqh", [P, NG, P], F32R)
        wql = sb("wql", [P, NG, P], F32R)
        wkh = sb("wkh", [P, NG, P], F32R)
        wkl = sb("wkl", [P, NG, P], F32R)
        wvT = sb("wvT", [P, H * DH])
        woT = sb("woT", [P, D])
        rwf = sb("rwf", [P, E])
        rwh = sb("rwh", [P, E], F32R)
        rwl = sb("rwl", [P, E], F32R)
        cst = sb("cst", [P, C_END])
        bqk = sb("bqk", [P, 2 * NG])
        nwb = sb("nwb", [P, D])
        cbb = sb("cbb", [P, D])
        small = sb("small", [P, 64])
        ones = sb("ones", [1, P])
        wexp = sb("wexp", [P, B * TPB * E])
        hb = sb("hb", [P, TPK, D])

        ident = cst[:, C_ID:C_ID + P]
        nmq, nmk = cst[:, C_NMQ:C_NMQ + 1], cst[:, C_NMK:C_NMK + 1]
        iota = cst[:, C_IOTA:C_ONE]
        one = cst[:, C_ONE:C_END].rearrange("p (a b c) -> p a b c", a=1, b=1)
        relu_b, sq_b = PB[:, 0], PB[:, 1]
        hTa = PB[:].rearrange("p a j n -> p (a j n)")
        w_om = SC[:]
        ob = SC[:, 0:1024].rearrange("p (t c) -> p t c", c=P)
        oT2 = SC[:, 1024:2048]
        MX = SC[:, 2048:2560].rearrange("p (t c) -> p t c", c=P)
        accS = SC[:, 2560:3072]
        qf = SC[:, 3072:4096].rearrange("p (u n) -> p u n", u=2)
        tA = SC[:, 0:1024].rearrange("p (u n) -> p u n", u=2)
        sqA = SC[:, 1024:1536]
        Vst = VH[:, 0:1024]
        hf = VH[:, 1024:2048].rearrange("p (u n) -> p u n", u=2)
        w1f = VH[:]
        wqf = Vg[:].rearrange("p a t j r -> p (a t j r)")[:, 0:2 * NG * P]

        st = sb("st", [P, TPK, 6])
        mv = sb("mv", [P, TPK, 2])
        ve = sb("ve", [P, TPK])
        rs = sb("rs", [P, TPK])
        nt = sb("nt", [P, TPK])
        ssq = sb("ssq", [P, NBLK * TPK])
        ve2 = sb("ve2", [P, TPK])
        rs2 = sb("rs2", [P, TPK])
        hsum = sb("hsum", [P, NBLK])
        hm = sb("hm", [P, B])
        lgT = sb("lgT", [E, BLK])
        lg = sb("lg", [P, TPK, E])
        m8 = sb("m8", [P, TPK, 8])
        ix = sb("ix", [P, TPK, 8], U32)
        ixf = sb("ixf", [P, TPK, 2])
        dd = sb("dd", [P, TPK])
        ed = sb("ed", [P, TPK])
        eds = sb("eds", [P, TPK])
        pr = sb("pr", [P, 2, TPK])
        wa = sb("wa", [P, TPK, E])
        wb = sb("wb", [P, TPK, E])
        mxp = sb("mxp", [P, TPB, HG])
        rc = sb("rc", [P, TPK, HG])
        vgf = Vg[:].rearrange("p a t j r -> p (a t j r)")
        Ub = vgf[0:OD, 1024:1280].rearrange("p (b j) -> p b j", b=B)
        Nn = SC[0:OD, 2560:2816].rearrange("p (b j) -> p b j", b=B)
        Wout = vgf[0:OD, 1280:1408]
        Wouth = vgf[0:OD, 1408:1536]
        Mg = SC[:, 1536:2048].rearrange("p (b d) -> p b d", b=B)
        wpi = vgf[:, 1536:1600]
        wpo = vgf[0:VD, 1600:1728]
        code = vgf[0:VC, 1728:1792]
        coden = vgf[0:VC, 1792:1856]
        bpb = vgf[0:B, 1856:1920]
        crow = SC[0:1, 2048:2560].rearrange("p (b d) -> p b d", b=B)
        row = lgT[0:1, :].rearrange("p (k d) -> p k d", k=4)
        cbrow = vgf[0:1, 1920:2048]
        bpc = sb("bpc", [VD, 1])
        v4 = sb("v4", [B, VD])
        v4n = sb("v4n", [B, VD])
        vT = sb("vT", [VD, B])
        vqT = sb("vqT", [VD, B])
        vnT = sb("vnT", [VD, B])
        cnT = sb("cnT", [VD, VC])
        ssn = sb("ssn", [VC, 2])
        rsn = sb("rsn", [VC, 2])
        ntn = sb("ntn", [VC, 2])
        sc4 = sb("sc4", [B, VC])
        m84 = sb("m84", [B, 8])
        ix4 = sb("ix4", [B, 8], U32)
        if4 = sb("if4", [B, 1])
        oh = sb("oh", [B, VC])
        ohT = sb("ohT", [VC, B])
        pad = sb("pad", [1, 1])
        bvc = sb("bvc", [P, 1])
        mix = small[:, 0:1]
        vqm = small[:, 1:2]

        six = ps("six", [P, 6, BLK])
        big, s1 = six[:, 0:4], six[:, 4:6]
        se = six[:, 0:2]
        sm = six[:, 2:6].rearrange("p (r a) n -> p r (a n)", a=2)
        acc = ps("acc", [P, BLK])
        misc = ps("misc", [P, BLK])

        S = {n: sem(n) for n in (
            "x0_loaded", "x1_loaded", "x2_loaded", "x3_loaded", "cst_loaded", "w1_loaded", "w2_loaded",
            "wom_loaded", "vq_loaded", "attw_loaded", "wqk_loaded", "ub_loaded", "bu_loaded",
            "dve_step", "h_ready", "lnt_done", "ht_ready", "hlo_ready",
            "w1_split", "rw_split", "wqk_split", "km_zeroed", "pool_zeroed", "fills_done",
            "hm_ready", "vqp_done", "par_done", "par_taken", "ubt_done", "nn_ready", "om_done", "om_taken",
            "cn_ready", "cnt_done", "cnt_taken", "vsc_done", "oh_ready", "oht_done", "oht_taken", "code_done",
            "vq_ready", "crow_done", "crow_ready", "mg_ready", "cb_ready", "cbr_done", "cbr_taken", "cbb_done",
            "cbb_ready", "a2_done", "a2_sq", "t_ready", "x1_ready",
            "router_done", "lgt_stored", "lg_done", "lg_taken", "d_ready", "ed_ready",
            "hid_done", "relu_done", "sqv_done", "sqa_done", "y_done", "comb_done",
            "s2_done", "s1_done", "pv_done", "exp_done", "max_done", "acc_stored",
            "qkp_done", "qkp_taken", "qk_split", "km_stored", "mx_ready", "mxt_done", "q_shifted",
            "ot_done", "o_normed", "obt_done", "obt_stored", "wo_done", "x_added", "x_biased",
            "v_done", "v_stored", "vg_ready", "out_stored", "mx_zeroed")}
        G_ = S.__getitem__
        x_loaded = [G_(f"x{b}_loaded") for b in range(B)]

        block = ctx.enter_context(nc.Block())

        def ln_count(kind, n):
            return NBLK * kind + n + 1

        @block.sync
        def _(sp):
            xv = a["x"].rearrange("b (p i) d -> p b (i d)", p=P)
            for b in range(B):
                sp.dma_start(x[:, b * L:(b + 1) * L], xv[:, b, :]).then_inc(x_loaded[b], 16)
                if b == 0:
                    sp.dma_start(cst[:], a["cst"]).then_inc(G_("cst_loaded"), 16)
            sp.dma_start(w1f.rearrange("p (e h) -> p e h", e=E),
                         a["w1"].rearrange("e d h -> d e h")).then_inc(G_("w1_loaded"), 16)
            sp.dma_start(w_om, a["w_om"]).then_inc(G_("wom_loaded"), 16)
            for dst, src in ((Wout, a["woutT"]), (wpi, a["wpiT"]), (wpo, a["wpoT"]), (code, a["cb"]),
                             (row[0:1, 0, :], a["bpo"]), (row[0:1, 1, :], a["bout"]), (row[0:1, 2, :], a["bo"]),
                             (bpc[:], a["bpi"].rearrange("a n -> n a")), (bpb, a["bpi"].broadcast_to([B, VD])),
                             (mix, a["mix"].broadcast_to([P, 1])), (vqm, a["vqm"].broadcast_to([P, 1])),
                             (nwb[:], a["nw"].broadcast_to([P, D])), (bvc[:], a["bv"].rearrange("a n -> n a"))):
                sp.dma_start(dst, src).then_inc(G_("vq_loaded"), 16)
            for dst, src in ((wqf[:, 0:NG * P], a["wqs"]), (wqf[:, NG * P:2 * NG * P], a["wks"]),
                             (rwf[:], a["rwT"])):
                sp.dma_start(dst, src).then_inc(G_("wqk_loaded"), 16)
            for dst, src in ((wvT[:], a["wvT"]), (woT[:], a["woT"]), (bqk[:, 0:NG], a["bqs"]),
                             (bqk[:, NG:2 * NG], a["bks"])):
                sp.dma_start(dst, src).then_inc(G_("attw_loaded"), 16)
            sp.dma_start(w2s[:], a["w2"].rearrange("e (c h) d -> h (e c) d", c=CH)).then_inc(G_("w2_loaded"), 16)
            for hv in range(2):
                if hv == 0:
                    sp.wait_ge(G_("w1_split"), 2)
                else:
                    sp.wait_ge(G_("ub_loaded"), 16 * B)
                sp.dma_start(VH[32:32 + B, :], a["b_om"][:, hv * OMEGA_HALF:(hv + 1) * OMEGA_HALF]
                             .broadcast_to([B, OMEGA_HALF])).then_inc(G_("bu_loaded"), 16)
                sp.wait_ge(G_("par_taken"), 4 * (hv + 1))
                for b in range(B):
                    sp.dma_start(Ub[hv * 32:(hv + 1) * 32, b, :],
                                 VH[b:b + 1, :].rearrange("o (i j) -> o i j", j=OD)
                                 ).then_inc(G_("ub_loaded"), 16)

            def spread_keys(done, g):
                for half in range(2):
                    sp.wait_ge(G_("qk_split"), 4 * done + 3 + half)
                    for j in range(HG):
                        sp.dma_start(Km[RB * j:RB * (j + 1), g, j, half * BLK:(half + 1) * BLK].bitcast(F32),
                                     Kst[RB * j:RB * (j + 1), :].bitcast(F32)).then_inc(G_("km_stored"), 16)

            sp.wait_ge(G_("km_zeroed"), 1)
            spread_keys(0, 0)
            spread_keys(1, 1)
            with sp.Fori(0, B - 1) as b:
                for g in range(NG):
                    spread_keys(4 * b + g + 2, (g + 2) % NG)
            spread_keys(4 * (B - 1) + 2, 2)
            spread_keys(4 * (B - 1) + 3, 3)

            ov = out.rearrange("b (p u i) d -> p b u (i d)", p=P, u=2)
            with sp.Fori(0, B) as b:
                for u in range(2):
                    sp.wait_ge(G_("comb_done"), E * (NBLK + 2 * b + u + 1))
                    sp.dma_start(ov[:, ds(b, 1), u, :], x[:, ds(b * L + u * BLK, BLK)]
                                 .rearrange("p (o n) -> p o n", o=1)).then_inc(G_("out_stored"), 16)
            sp.wait_ge(G_("out_stored"), 16 * NBLK)

        @block.gpsimd
        def _(pl):
            pl.memset(ones[0:1, :], 1.0).then_inc(G_("fills_done"), 1)
            pl.wait_ge(G_("cst_loaded"), 16)
            pl.wait_ge(G_("w1_loaded"), 16)
            pl.tensor_copy(w1h[:], w1f).then_inc(G_("w1_split"), 1)
            pl.wait_ge(G_("w1_split"), 1)
            pl.tensor_tensor(w1l[:], w1f, w1h[:].bitcast(F32), ALU.subtract).then_inc(G_("w1_split"), 1)
            pl.wait_ge(G_("wqk_loaded"), 48)
            pl.tensor_copy(rwh[:], rwf[:]).then_inc(G_("rw_split"), 1)
            pl.wait_ge(G_("rw_split"), 1)
            pl.tensor_tensor(rwl[:], rwf[:], rwh[:].bitcast(F32), ALU.subtract).then_inc(G_("rw_split"), 1)

            for g in range(NG):
                ins = pl.memset(Km[:, g].bitcast(F32), 0.0)
            ins.then_inc(G_("km_zeroed"), 1)

            def residual_add(n):
                pl.wait_ge(G_("t_ready"), n + 1)
                pl.tensor_tensor(x[:, n * BLK:(n + 1) * BLK], x[:, n * BLK:(n + 1) * BLK], tA[:, n % 2, :],
                                 ALU.add).then_inc(G_("x1_ready"), 1)

            for n in range(NBLK):
                residual_add(n)

            def low_part(kind, n):
                m = NBLK * (kind - 1) + n + 1
                pl.wait_ge(G_("ht_ready"), ln_count(kind, n))
                pl.tensor_tensor(hTl[:, ds((n % 4) * BLK, BLK)], hf_block(n), hTh[:, ds((n % 4) * BLK, BLK)]
                                 .bitcast(F32), ALU.subtract).then_inc(G_("hlo_ready"), 1)
                return m

            def hf_block(n):
                return VH[:, ds(1024 + (n % 2) * BLK, BLK)]

            low_part(1, 0)
            low_part(1, 1)
            wq4 = wqf.rearrange("p (a g c) -> p a g c", a=2, g=NG)
            for s, (hi, lo) in enumerate(((wqh, wql), (wkh, wkl))):
                pl.tensor_copy(hi[:], wq4[:, s]).then_inc(G_("wqk_split"), 1)
                pl.wait_ge(G_("wqk_split"), 2 * s + 1)
                pl.tensor_tensor(lo[:], wq4[:, s], hi[:].bitcast(F32), ALU.subtract).then_inc(G_("wqk_split"), 1)
            pl.wait_ge(G_("wqk_split"), 4)
            pl.memset(Vg[:], 0.0).then_inc(G_("pool_zeroed"), 1)
            pl.memset(MX, 0.0).then_inc(G_("mx_zeroed"), 1)
            pl.wait_ge(G_("pool_zeroed"), 1)
            pl.memset(Vg[:, :, :, :, DH:DH + 1], 1.0).then_inc(G_("pool_zeroed"), 1)
            with pl.Fori(2, NBLK) as n:
                low_part(1, n)

            def bias_block(n):
                pl.wait_ge(G_("h_ready"), ln_count(2, n))
                xb = x[:, ds(n * BLK, BLK)].rearrange("p (t c) -> p t c", c=D)
                pl.tensor_tensor(xb, xb, cbb[:].rearrange("p (o c) -> p o c", o=1).broadcast_to([P, TPK, D]),
                                 ALU.add).then_inc(G_("x_biased"), 1)

            def group_values(g):
                v = Vst.rearrange("p (t h d) -> p t h d", t=TPB, d=DH)[:, :, HG * g:HG * (g + 1), :]
                pl.tensor_tensor(Vg[:, g % 2, :, :, 0:DH], v, one.broadcast_to([P, TPB, HG, DH]), ALU.mult).then_inc(G_("vg_ready"), 1)

            low_part(2, 0)
            low_part(2, 1)
            pl.wait_ge(G_("v_stored"), 2)
            pl.wait_ge(G_("pool_zeroed"), 2)
            group_values(0)
            pl.wait_ge(G_("cbb_ready"), 1)
            bias_block(0)
            bias_block(1)

            def attention_batch(b, last):
                group_values(1)
                if not last:
                    for u in range(2):
                        low_part(2, 2 * b + 2 + u)
                        bias_block(2 * b + 2 + u)
                for g in (2, 3):
                    pl.wait_ge(G_("pv_done"), BSTEPS * b + STEPS * (g - 1))
                    group_values(g)
                if not last:
                    pl.wait_ge(G_("v_stored"), 2 * b + 4)
                    pl.wait_ge(G_("pv_done"), BSTEPS * b + STEPS * 3)
                    group_values(0)
                pl.wait_ge(G_("pv_done"), BSTEPS * b + BSTEPS)

            with pl.Fori(0, B - 1) as b:
                attention_batch(b, False)
            attention_batch(B - 1, True)

            low_part(3, 0)
            with pl.Fori(1, NBLK) as n:
                low_part(3, n)

        @block.scalar
        def _(act):
            for n in range(NBLK):
                act.wait_ge(G_("lnt_done"), ln_count(0, n))
                act.activation(hTa[:, n * BLK:(n + 1) * BLK], misc[:], ACT.Copy,
                               accum_out=hsum[:, n:n + 1]).then_inc(G_("ht_ready"), 1)
            for n in range(NBLK):
                act.wait_ge(G_("a2_done"), n + 1)
                if n:
                    act.wait_ge(G_("a2_sq"), n)
                for i in range(TPK):
                    ins = act.activation(sqA[:, i * D:(i + 1) * D], big[:, n % 4, i * P:(i + 1) * P], ACT.Square,
                                         accum_out=ssq[:, n * TPK + i:n * TPK + i + 1])
                ins.then_inc(G_("a2_sq"), 1)

            def ht_out(kind, n, guard=None):
                act.wait_ge(G_("lnt_done"), ln_count(kind, n))
                if guard is not None:
                    act.wait_ge(*guard)
                act.activation(VH[:, ds(1024 + (n % 2) * BLK, BLK)], misc[:], ACT.Copy)
                act.activation(hTh[:, ds((n % 4) * BLK, BLK)], misc[:], ACT.Copy).then_inc(G_("ht_ready"), 1)

            def lo_free(kind, n):
                return G_("hlo_ready"), NBLK * (kind - 1) + n - 1

            def experts_block(f, n, last):
                N = NBLK * f + n
                act.wait_ge(G_("router_done"), N + 1)
                act.activation(lgT[:], s1[0:E, 0, :], ACT.Copy).then_inc(G_("lgt_stored"), 1)
                for e in range(E):
                    for c in range(CH):
                        q = CH * e + c
                        act.wait_ge(G_("hid_done"), CH * E * N + q + 1)
                        if c == 0 and not (f == 0 and n_is(n, 0) and e < 2):
                            act.wait_ge(G_("sqv_done"), E * N + e - 1)
                        act.activation(relu_b[:, q % 4, :], big[:, q % 2, :], ACT.Relu
                                       ).then_inc(G_("relu_done"), 1)
                    act.wait_ge(G_("relu_done"), CH * E * N + CH * e + 2)
                    if not (f == 0 and n_is(n, 0) and e < 2):
                        act.wait_ge(G_("y_done"), E * N + e - 1)
                    act.activation(sq_b[:, 2 * (e % 2) + 1, :], relu_b[:, (CH * e + 1) % 4, :], ACT.Square
                                   ).then_inc(G_("sqa_done"), 1)
                    if e == 1:
                        act.wait_ge(G_("d_ready"), N + 1)
                        act.activation(ed[:], dd[:], ACT.Exp).then_inc(G_("ed_ready"), 1)
                    if e == 6 and not last:
                        ht_out(2 * f + 1, n + 1, lo_free(2 * f + 1, n + 1))

            def n_is(n, v):
                return isinstance(n, int) and n == v

            def experts(f):
                kind = 2 * f + 1
                if f == 0:
                    act.wait_ge(G_("par_done"), 8)
                    act.wait_ge(G_("ub_loaded"), 32 * B)
                    ht_out(kind, 0)
                else:
                    ht_out(kind, 0, (G_("v_done"), 2 * B))
                experts_block(f, 0, False)
                with act.Fori(1, NBLK - 1) as n:
                    experts_block(f, n, False)
                experts_block(f, NBLK - 1, True)

            experts(0)

            def proj_out(count, task, g):
                u = task % 2
                act.wait_ge(G_("qkp_done"), count + task + 1)
                if not (isinstance(count, int) and count + task < 1):
                    act.wait_ge(G_("qk_split"), count + task)
                bias = bqs[:, g:g + 1] if task < 2 else bqk[:, NG + g:NG + g + 1]
                scale = DH ** -0.5 if task < 2 else 1.0
                act.activation(qf[:, u, :], misc[:], ACT.Identity, bias=bias, scale=scale)
                act.activation(tr[:], misc[:], ACT.Identity, bias=bias, scale=scale
                               ).then_inc(G_("qkp_taken"), 1)

            def v_out(count, r):
                act.wait_ge(G_("v_done"), count + r + 1)
                act.activation(Vst[:, r * BLK:(r + 1) * BLK], misc[:], ACT.Copy).then_inc(G_("v_stored"), 1)

            bqs = small[:, 8:8 + NG]
            act.wait_ge(G_("attw_loaded"), 64)
            act.activation(bqs, bqk[:, 0:NG], ACT.Copy, scale=DH ** -0.5).then_inc(G_("cb_ready"), 1)
            act.wait_ge(G_("cb_ready"), 1)
            ht_out(2, 0)
            ht_out(2, 1)
            for t in range(4):
                proj_out(0, t, 0)
            for r in range(2):
                v_out(0, r)
            for t in range(4):
                proj_out(4, t, 1)

            def output_rows(b, r):
                act.wait_ge(G_("obt_done"), 2 * b + r + 1)
                act.activation(oT2[:, r * BLK:(r + 1) * BLK], misc[:], ACT.Copy).then_inc(G_("obt_stored"), 1)

            def attention_batch(b, first, last):
                for k in range(BSTEPS):
                    g, kk = divmod(k, STEPS)
                    for j in range(HG):
                        act.wait_ge(G_("s2_done"), HG * (BSTEPS * b + k) + j + 1)
                        if j == 0 and not (first and k < 2):
                            act.wait_ge(G_("pv_done"), BSTEPS * b + k - 1)
                        act.activation(PB[:, k % 2, j, :], se[:, j % 2, :], ACT.Exp).then_inc(G_("exp_done"), 1)
                    if kk in (0, 8) and k > 0:
                        acc_out(b, k // 8 - 1, first)
                    if k == 0 and not first:
                        acc_out(b - 1, 7)
                    if k in (3, 8) and not first:
                        output_rows(b - 1, k // 8)
                    if kk in (4, 5, 6, 7) and not (last and g >= 2):
                        proj_out(4 * (4 * b + g + 2), kk - 4, (g + 2) % NG)
                    if not last and g == 3 and kk in (9, 10):
                        if kk == 9:
                            act.wait_ge(G_("vg_ready"), 4 * b + 4)
                        v_out(2 * b + 2, kk - 9)
                    if not last and g in (0, 1) and kk == 14:
                        ht_out(2, 2 * b + 2 + g, (G_("hlo_ready"), NBLK + 2 * b + 1 + g))

            def acc_out(b, i, first=False):
                act.wait_ge(G_("pv_done"), BSTEPS * b + 8 * (i + 1))
                if not (first and i == 0):
                    act.wait_ge(G_("ot_done"), 8 * b + i)
                act.activation(accS, acc[:], ACT.Copy).then_inc(G_("acc_stored"), 1)

            attention_batch(0, True, False)
            with act.Fori(1, B - 1) as b:
                attention_batch(b, False, False)
            attention_batch(B - 1, False, True)
            acc_out(B - 1, 7)
            for r in range(2):
                output_rows(B - 1, r)
            experts(1)

        @block.vector
        def _(dve):
            link = Chain(dve, G_("dve_step"))

            def rsqrt(v, y, t):
                yi = y.bitcast(I32)
                link(dve.tensor_scalar(yi, v.bitcast(I32), 1, None, ALU.arith_shift_right))
                link(dve.tensor_scalar(yi, yi, -1.0, RSQRT_MAGIC, ALU.mult, ALU.add))
                for _ in range(3):
                    link(dve.tensor_tensor(t, y, y, ALU.mult))
                    link(dve.scalar_tensor_tensor(out=t, in0=t, scalar=-0.5, in1=v, op0=ALU.mult, op1=ALU.mult))
                    link(dve.scalar_tensor_tensor(out=y, in0=t, scalar=1.5, in1=y, op0=ALU.add, op1=ALU.mult))

            def ln_stats(n):
                for i in range(TPK):
                    ins = dve.bn_stats(st[:, i, :], x[:, ds(n * BLK + i * D, D)])
                link(ins)
                dve.memset(pad[:], 0.0)
                for i in range(TPK):
                    ins = dve.bn_aggr(mv[:, i, :], st[:, i, :])
                link(ins)
                link(dve.tensor_scalar(ve[:], mv[:, :, 1], LN_EPS, None, ALU.add))

            def ln_norm(kind, n, first=False):
                if not first:
                    dve.wait_ge(G_("lnt_done"), ln_count(kind, n) - 1)
                for i in range(TPK):
                    ins = dve.tensor_scalar(hb[:, i, :], x[:, ds(n * BLK + i * D, D)], mv[:, i, 0:1],
                                            rs[:, i:i + 1], ALU.subtract, ALU.mult)
                ins.then_inc(G_("h_ready"), 1)

            def layer_norm(kind, n, first=False):
                ln_stats(n)
                rsqrt(ve[:], rs[:], nt[:])
                ln_norm(kind, n, first)

            for n in range(NBLK):
                if n % 2 == 0:
                    dve.wait_ge(x_loaded[n // 2], 16)
                layer_norm(0, n, first=(n == 0))

            dve.wait_ge(G_("ht_ready"), NBLK)
            dve.wait_ge(G_("cst_loaded"), 16)
            dve.wait_ge(G_("vq_loaded"), 13 * 16)
            hs2 = hsum[:].rearrange("p (b u) -> p b u", u=2)
            link(dve.tensor_tensor(hm[:], hs2[:, :, 0], hs2[:, :, 1], ALU.add))
            dve.tensor_scalar(hm[:], hm[:], 1.0 / L, None, ALU.mult).then_inc(G_("hm_ready"), 1)
            for c in range(8):
                if c % 4 == 0:
                    dve.wait_ge(G_("bu_loaded"), 16 * (c // 4 + 1))
                dve.wait_ge(G_("par_done"), c + 1)
                cols = slice((c % 4) * BLK, (c % 4 + 1) * BLK)
                dve.tensor_tensor(VH[0:B, cols], big[0:B, c % 4, :], VH[32:32 + B, cols], ALU.add
                                  ).then_inc(G_("par_taken"), 1)
            link(dve.tensor_tensor(coden, code, code, ALU.mult))
            link(dve.memset(ssn[:], 1.0))
            link(dve.reduce_sum(ssn[:, 0:1], coden, AX.X))
            dve.wait_ge(G_("vqp_done"), 1)
            link(dve.tensor_tensor(v4[:], s1[0:B, 0, 64:128], bpb, ALU.add))
            link(dve.tensor_scalar(vT[:], s1[0:VD, 0, 0:B], bpc[:, 0:1], None, ALU.add))
            link(dve.tensor_tensor(v4n[:], v4[:], v4[:], ALU.mult))
            link(dve.reduce_sum(ssn[0:B, 1:2], v4n[:], AX.X))
            rsqrt(ssn[:], rsn[:], ntn[:])
            link(dve.tensor_scalar(rsn[:], rsn[:], 1.0 / NORM_EPS, None, ALU.min))
            dve.tensor_scalar(coden, code, rsn[:, 0:1], None, ALU.mult)
            dve.tensor_scalar(v4n[:], v4[:], rsn[0:B, 1:2], None, ALU.mult).then_inc(G_("cn_ready"), 1)
            dve.wait_ge(G_("cnt_done"), 1)
            dve.tensor_copy(cnT[:], s1[0:VD, 1, 0:VC])
            dve.tensor_copy(vnT[:], s1[0:VD, 1, VC:VC + B]).then_inc(G_("cnt_taken"), 1)
            dve.wait_ge(G_("vsc_done"), 1)
            link(dve.tensor_copy(sc4[:], s1[0:B, 1, 64:64 + VC]))
            link(dve.max(m84[:], sc4[:]))
            link(dve.max_index(ix4[:], m84[:], sc4[:]))
            link(dve.tensor_copy(if4[:], ix4[:, 0:1]))
            dve.tensor_scalar(oh[:], iota[0:B, :], if4[:, 0:1], None, ALU.is_equal).then_inc(G_("oh_ready"), 1)
            dve.wait_ge(G_("oht_done"), 1)
            dve.tensor_copy(ohT[:], s1[0:VC, 1, 128:128 + B]).then_inc(G_("oht_taken"), 1)
            dve.wait_ge(G_("code_done"), 1)
            link(dve.tensor_tensor(vqT[:], s1[0:VD, 1, 160:160 + B], vT[:], ALU.subtract))
            dve.tensor_tensor(vqT[:], vqT[:], vT[:], ALU.add).then_inc(G_("vq_ready"), 1)
            link(dve.tensor_scalar(row[0:1, 3, :], row[0:1, 1, :], mix[0:1, :], None, ALU.mult))
            dve.wait_ge(G_("crow_done"), 1)

            def over_b(ap):
                return ap.broadcast_to([ap.shape[0], B, D])

            link(dve.tensor_tensor(crow, s1[0:1, 0, :].rearrange("p (b d) -> p b d", b=B),
                                   over_b(row[0:1, 0:1, :]), ALU.add))
            dve.scalar_tensor_tensor(out=crow, in0=crow, scalar=vqm[0:1, :], in1=over_b(row[0:1, 3:4, :]),
                                     op0=ALU.mult, op1=ALU.add).then_inc(G_("crow_ready"), 1)
            link(dve.tensor_scalar(Wouth, Wout, 0.5, None, ALU.mult))
            dve.wait_ge(G_("ubt_done"), 1)
            dve.tensor_tensor(Nn[:], misc[0:OD, 0:B * OD].rearrange("p (b j) -> p b j", b=B), Ub,
                              ALU.subtract).then_inc(G_("nn_ready"), 1)
            for s in range(3):
                dve.wait_ge(G_("om_done"), s + 1)
                z = acc[0:OD, :].rearrange("p (b d) -> p b d", b=B)
                y = Mg[0:OD]
                if s == 0:
                    dve.scalar_tensor_tensor(out=y, in0=z, scalar=1.0 / 6.0, in1=over_b(Wouth.rearrange(
                        "p (o d) -> p o d", o=1)), op0=ALU.mult, op1=ALU.add).then_inc(G_("om_taken"), 1)
                elif s == 1:
                    dve.tensor_tensor(y, z, over_b(Wout.rearrange("p (o d) -> p o d", o=1)), ALU.add
                                      ).then_inc(G_("om_taken"), 1)
                else:
                    link(dve.tensor_tensor(y, z, over_b(Wout.rearrange("p (o d) -> p o d", o=1)), ALU.add))
            idb = ident.rearrange("p (o d) -> p o d", o=1)
            dve.tensor_copy(Mg[OD:P], over_b(idb[OD:P]))
            dve.scalar_tensor_tensor(out=Mg[0:OD], in0=Mg[0:OD], scalar=mix[0:OD, :], in1=over_b(idb[0:OD]),
                                     op0=ALU.mult, op1=ALU.add).then_inc(G_("mg_ready"), 1)
            dve.wait_ge(G_("cbr_done"), 1)
            dve.tensor_tensor(cbrow, s1[0:1, 1, 256:256 + D], row[0:1, 2, :], ALU.add
                              ).then_inc(G_("cbr_taken"), 1)
            dve.wait_ge(G_("cbb_done"), 1)
            dve.tensor_copy(cbb[:], s1[:, 0, 0:D]).then_inc(G_("cbb_ready"), 1)

            for n in range(NBLK):
                dve.wait_ge(G_("a2_sq"), n + 1)
                link(dve.tensor_scalar(ve2[:], ssq[:, n * TPK:(n + 1) * TPK], 1.0 / D, RMS_EPS, ALU.mult, ALU.add))
                rsqrt(ve2[:], rs2[:], nt[:])
                if n >= 2:
                    dve.wait_ge(G_("x1_ready"), n - 1)
                for i in range(TPK):
                    ins = dve.scalar_tensor_tensor(out=tA[:, n % 2, i * D:(i + 1) * D],
                                                   in0=big[:, n % 4, i * D:(i + 1) * D], scalar=rs2[:, i:i + 1],
                                                   in1=nwb[:], op0=ALU.mult, op1=ALU.mult)
                ins.then_inc(G_("t_ready"), 1)

            def n_is(n, v):
                return isinstance(n, int) and n == v

            def add_expert(f, n, e):
                N = NBLK * f + n
                dve.wait_ge(G_("y_done"), E * N + e + 1)
                if not (f == 0 and n_is(n, 0) and e == 0):
                    dve.wait_ge(G_("comb_done"), E * N + e)
                for i in range(TPK):
                    xt = x[:, ds(n * BLK + i * D, D)]
                    ins = dve.scalar_tensor_tensor(out=xt, in0=big[:, 2 + e % 2, i * D:(i + 1) * D],
                                                   scalar=wexp[:, ds((n * TPK + i) * E + e, 1)], in1=xt,
                                                   op0=ALU.mult, op1=ALU.add)
                ins.then_inc(G_("comb_done"), 1)

            def top_two(N):
                dve.wait_ge(G_("lg_done"), N + 1)
                dve.tensor_copy(lg[:], s1[:, 1, 0:TPK * E].rearrange("p (t e) -> p t e", e=E)
                                ).then_inc(G_("lg_taken"), 1)
                dve.wait_ge(G_("lg_taken"), N + 1)
                dve.memset(pad[:], 0.0)
                for i in range(TPK):
                    ins = dve.max(m8[:, i, :], lg[:, i, :])
                link(ins)
                dve.tensor_tensor(dd[:], m8[:, :, 1], m8[:, :, 0], ALU.subtract).then_inc(G_("d_ready"), 1)
                for i in range(TPK):
                    ins = dve.max_index(ix[:, i, :], m8[:, i, :], lg[:, i, :])
                link(ins)
                link(dve.tensor_copy(ixf[:], ix[:, :, 0:2]))

            def expert_weights(N, n):
                dve.wait_ge(G_("ed_ready"), N + 1)
                link(dve.tensor_scalar(eds[:], ed[:], 1.0, None, ALU.add))
                link(dve.reciprocal(pr[:, 0, :], eds[:]))
                link(dve.tensor_tensor(pr[:, 1, :], ed[:], pr[:, 0, :], ALU.mult))
                io = iota[:, 0:E].rearrange("p (o e) -> p o e", o=1).broadcast_to([P, TPK, E])
                for s, w in enumerate((wa, wb)):
                    ins = dve.tensor_tensor(w[:], io, ixf[:, :, s:s + 1].broadcast_to([P, TPK, E]), ALU.is_equal)
                link(ins)
                for s, w in enumerate((wa, wb)):
                    ins = dve.tensor_tensor(w[:], w[:], pr[:, s, :].rearrange("p (t o) -> p t o", o=1)
                                            .broadcast_to([P, TPK, E]), ALU.mult)
                link(ins)
                link(dve.tensor_tensor(wexp[:, ds(n * TPK * E, TPK * E)], wa[:].rearrange("p t e -> p (t e)"),
                                       wb[:].rearrange("p t e -> p (t e)"), ALU.add))

            def experts_block(f, n, last):
                N = NBLK * f + n
                for e in range(E):
                    dve.wait_ge(G_("relu_done"), CH * E * N + CH * e + 1)
                    if not (f == 0 and n_is(n, 0) and e < 2):
                        dve.wait_ge(G_("y_done"), E * N + e - 1)
                    rl = relu_b[:, (CH * e) % 4, :]
                    dve.tensor_tensor(sq_b[:, 2 * (e % 2), :], rl, rl, ALU.mult).then_inc(G_("sqv_done"), 1)
                    if e == 0 and not n_is(n, 0):
                        add_expert(f, n - 1, E - 1)
                    if e == 1:
                        top_two(N)
                    if e == 2:
                        expert_weights(N, n)
                        add_expert(f, n, 0)
                    if e >= 2:
                        add_expert(f, n, e - 1)
                    if not last and e == 3:
                        if f == 0:
                            dve.wait_ge(G_("x1_ready"), NBLK)
                        ln_stats(n + 1)
                    if not last and e == 4:
                        rsqrt(ve[:], rs[:], nt[:])
                    if not last and e == 5:
                        ln_norm(2 * f + 1, n + 1)

            def experts(f):
                if f == 0:
                    dve.wait_ge(G_("x1_ready"), 1)
                layer_norm(2 * f + 1, 0)
                experts_block(f, 0, False)
                with dve.Fori(1, NBLK - 1) as n:
                    link.enter(n - 1, FFN_CHAIN)
                    experts_block(f, n, False)
                    link.leave(NBLK - 2, FFN_CHAIN)
                experts_block(f, NBLK - 1, True)
                add_expert(f, NBLK - 1, E - 1)

            experts(0)

            def split_out(count, task, g):
                dve.wait_ge(G_("qkp_taken"), count + task + 1)
                u = task % 2
                if task < 2:
                    dst, mask = Q[:, g, u * BLK:(u + 1) * BLK], nmq
                else:
                    dst, mask = Kst[:], nmk
                    if not (isinstance(count, int) and count + task == 2):
                        dve.wait_ge(G_("km_stored"), km_before(count, task))
                dve.scalar_tensor_tensor(out=dst, in0=tr[:].bitcast(F32), scalar=mask, in1=qf[:, u, :],
                                         op0=ALU.mult, op1=ALU.add).then_inc(G_("qk_split"), 1)

            def km_before(count, task):
                return count * 32 + (task - 2) * 64

            def maxima(count, kk):
                for i in range(2):
                    t, j = kk // 2, 2 * (kk % 2) + i
                    dve.wait_ge(G_("s1_done"), count + 2 * kk + i + 1)
                    dve.reduce_max(mxp[:, t, j:j + 1], sm[:, i, :], AX.X).then_inc(G_("max_done"), 1)

            def minus_max(count, half):
                dve.wait_ge(G_("max_done"), count + STEPS * (half + 1))
                mh = MX.rearrange("p t (j r) -> p t j r", r=RB)
                mq = mxp[:, TPK * half:TPK * (half + 1)]
                link(dve.tensor_scalar(mh[:, :, :, 24].bitcast(F32R), mq, -1.0, None, ALU.mult))
                dve.scalar_tensor_tensor(out=mh[:, :, :, 25], in0=mq, scalar=-1.0, in1=mh[:, :, :, 24],
                                         op0=ALU.mult, op1=ALU.subtract).then_inc(G_("mx_ready"), 1)

            def shift_queries(count, g, half):
                dve.wait_ge(G_("mxt_done"), count + half + 1)
                qh = Q[:, g, half * BLK:(half + 1) * BLK]
                dve.tensor_tensor(qh, misc[:], qh.bitcast(F32), ALU.add).then_inc(G_("q_shifted"), 1)

            def normalise(b, i):
                g, u = i // 2, i % 2
                dve.wait_ge(G_("ot_done"), 8 * b + i + 1)
                o4 = misc[:].rearrange("p (t j r) -> p t j r", t=TPK, r=RB)
                link(dve.reciprocal(rc[:], o4[:, :, :, DH]))
                dst = ob[:, TPK * u:TPK * (u + 1), HG * DH * g:HG * DH * (g + 1)]
                dve.tensor_tensor(dst.rearrange("p t (j d) -> p t j d", d=DH), o4[:, :, :, 0:DH],
                                  rc[:].rearrange("p t (j o) -> p t j o", o=1).broadcast_to([P, TPK, HG, DH]),
                                  ALU.mult).then_inc(G_("o_normed"), 1)

            layer_norm(2, 0)
            layer_norm(2, 1)
            for t in range(4):
                split_out(0, t, 0)
            for t in range(4):
                split_out(4, t, 1)
            dve.wait_ge(G_("mx_zeroed"), 1)
            for kk in range(STEPS):
                maxima(0, kk)
                if kk == 7:
                    minus_max(0, 0)
            shift_queries(0, 0, 0)
            minus_max(0, 1)

            def add_output(b, r):
                dve.wait_ge(G_("wo_done"), 2 * b + r + 1)
                dve.wait_ge(G_("x_biased"), 2 * b + r + 1)
                xb = x[:, ds(b * L + r * BLK, BLK)]
                dve.tensor_tensor(xb, misc[:], xb, ALU.add).then_inc(G_("x_added"), 1)

            def attention_batch(b, first, last):
                for k in range(BSTEPS):
                    g, kk = divmod(k, STEPS)
                    more = not (last and g == 3)
                    nxt = 4 * b + g + 1
                    if k == 1 and not first:
                        normalise(b - 1, 7)
                    if kk == 2:
                        shift_queries(2 * (4 * b + g), g, 1)
                    if kk == 3 and g > 0:
                        normalise(b, 2 * g - 1)
                    if k in (9, 10) and not first:
                        add_output(b - 1, k - 9)
                    if kk == 11 and more:
                        shift_queries(2 * nxt, (g + 1) % NG, 0)
                    if kk == 12:
                        normalise(b, 2 * g)
                    if more:
                        maxima(2 * STEPS * nxt, kk)
                    if kk in (4, 5, 6, 7) and not (last and g >= 2):
                        split_out(4 * (4 * b + g + 2), kk - 4, (g + 2) % NG)
                    if kk == 8 and more:
                        minus_max(2 * STEPS * nxt, 0)
                    if kk == 15 and more:
                        minus_max(2 * STEPS * nxt, 1)
                    if not last and g in (0, 1):
                        n = 2 * b + 2 + g
                        if kk == 8:
                            ln_stats(n)
                        if kk == 10:
                            rsqrt(ve[:], rs[:], nt[:])
                        if kk == 12:
                            ln_norm(2, n)

            attention_batch(0, True, False)
            with dve.Fori(1, B - 1) as b:
                link.enter(b - 1, ATT_CHAIN)
                attention_batch(b, False, False)
                link.leave(B - 2, ATT_CHAIN)
            attention_batch(B - 1, False, True)
            normalise(B - 1, 7)
            for r in range(2):
                add_output(B - 1, r)
            dve.wait_ge(G_("x_added"), 2 * B)
            experts(1)

        @block.tensor
        def _(pe):
            def ln_transpose(kind, n):
                pe.wait_ge(G_("h_ready"), ln_count(kind, n))
                for i in range(TPK):
                    ins = pe.transpose(misc[:, i * P:(i + 1) * P], hb[:, i, :], ident)
                ins.then_inc(G_("lnt_done"), 1)

            pe.wait_ge(G_("cst_loaded"), 16)
            for n in range(NBLK):
                if n:
                    pe.wait_ge(G_("ht_ready"), n)
                ln_transpose(0, n)

            pe.wait_ge(G_("hm_ready"), 1)
            pe.wait_ge(G_("vq_loaded"), 13 * 16)
            pe.matmul(s1[0:VD, 0, 0:B], wpi, hm[:], start=True, stop=True)
            pe.matmul(s1[0:B, 0, 64:128], hm[:], wpi, start=True, stop=True).then_inc(G_("vqp_done"), 1)
            pe.wait_ge(G_("wom_loaded"), 16)
            for c in range(8):
                if c >= 4:
                    pe.wait_ge(G_("par_taken"), c - 3)
                pe.matmul(big[0:B, c % 4, :], hm[:], w_om[:, c * BLK:(c + 1) * BLK], start=True, stop=True
                          ).then_inc(G_("par_done"), 1)
            pe.wait_ge(G_("cn_ready"), 1)
            pe.transpose(s1[0:VD, 1, 0:VC], coden, ident[0:VC, 0:VC])
            pe.transpose(s1[0:VD, 1, VC:VC + B], v4n[:], ident[0:B, 0:B]).then_inc(G_("cnt_done"), 1)
            pe.wait_ge(G_("cnt_taken"), 1)
            pe.matmul(s1[0:B, 1, 64:64 + VC], vnT[:], cnT[:], start=True, stop=True).then_inc(G_("vsc_done"), 1)
            pe.wait_ge(G_("oh_ready"), 1)
            pe.transpose(s1[0:VC, 1, 128:128 + B], oh[:], ident[0:B, 0:B]).then_inc(G_("oht_done"), 1)
            pe.wait_ge(G_("oht_taken"), 1)
            pe.matmul(s1[0:VD, 1, 160:160 + B], code, ohT[:], start=True, stop=True).then_inc(G_("code_done"), 1)
            pe.wait_ge(G_("vq_ready"), 1)
            for b in range(B):
                ins = pe.matmul(s1[0:1, 0, b * D:(b + 1) * D], vqT[:, b:b + 1], wpo, start=True, stop=True)
            ins.then_inc(G_("crow_done"), 1)
            pe.wait_ge(G_("ub_loaded"), 32 * B)
            pe.wait_ge(G_("ht_ready"), NBLK)
            for b in range(B):
                ins = pe.transpose(misc[0:OD, b * OD:(b + 1) * OD], Ub[:, b, :], ident[0:OD, 0:OD])
            ins.then_inc(G_("ubt_done"), 1)
            pe.wait_ge(G_("nn_ready"), 1)
            for s in range(3):
                if s:
                    pe.wait_ge(G_("om_taken"), s)
                for b in range(B):
                    ins = pe.matmul(acc[0:OD, b * D:(b + 1) * D], Nn[:, b, :], Wout if s == 0 else Mg[0:OD, b, :],
                                    start=True, stop=True)
                ins.then_inc(G_("om_done"), 1)
            pe.wait_ge(G_("attw_loaded"), 64)
            pe.matmul(s1[0:1, 1, 256:256 + D], bvc[:], woT[:], start=True, stop=True).then_inc(G_("cbr_done"), 1)
            pe.wait_ge(G_("cbr_taken"), 1)
            pe.wait_ge(G_("crow_ready"), 1)
            pe.wait_ge(G_("fills_done"), 1)
            pe.matmul(s1[:, 0, 0:D], ones[0:1, :], cbrow, start=True, stop=True).then_inc(G_("cbb_done"), 1)

            pe.wait_ge(G_("mg_ready"), 1)
            for n in range(NBLK):
                if n >= 4:
                    pe.wait_ge(G_("t_ready"), n - 3)
                for i in range(TPK):
                    T = n * TPK + i
                    pe.matmul(big[:, n % 4, i * D:(i + 1) * D], hTa[:, T * P:(T + 1) * P], Mg[:, n // 2, :],
                              start=True, stop=False)
                    ins = pe.matmul(big[:, n % 4, i * D:(i + 1) * D], ones[0:1, :], crow[0:1, n // 2, :],
                                    start=False, stop=True)
                ins.then_inc(G_("a2_done"), 1)

            def n_is(n, v):
                return isinstance(n, int) and n == v

            def three(dst, wh, wl, hoff, width=BLK):
                hh, hl = hTh[:, ds(hoff, width)], hTl[:, ds(hoff, width)]
                pe.matmul(dst, wh, hh, start=True, stop=False)
                pe.matmul(dst, wl, hh, start=False, stop=False)
                return pe.matmul(dst, wh, hl, start=False, stop=True)

            def expert_out(N, e):
                pe.wait_ge(G_("sqv_done"), E * N + e + 1)
                pe.wait_ge(G_("sqa_done"), E * N + e + 1)
                if not (n_is(N, 0) and e < 2):
                    pe.wait_ge(G_("comb_done"), E * N + e - 1)
                for i in range(TPK):
                    for c in range(CH):
                        ins = pe.matmul(big[:, 2 + e % 2, i * D:(i + 1) * D],
                                        sq_b[:, 2 * (e % 2) + c, i * P:(i + 1) * P], w2s[:, CH * e + c, :],
                                        start=(c == 0), stop=(c == CH - 1))
                ins.then_inc(G_("y_done"), 1)

            def experts_block(f, n, last):
                N = NBLK * f + n
                hoff = (n % 4) * BLK
                pe.wait_ge(G_("hlo_ready"), 2 * NBLK * f + n + 1)
                three(s1[0:E, 0, :], rwh[:], rwl[:], hoff).then_inc(G_("router_done"), 1)
                for e in range(E):
                    if e == 1:
                        pe.wait_ge(G_("lgt_stored"), N + 1)
                        if not n_is(N, 0):
                            pe.wait_ge(G_("lg_taken"), N)
                    for c in range(CH):
                        q = CH * e + c
                        if not (n_is(N, 0) and q < 2):
                            pe.wait_ge(G_("relu_done"), CH * E * N + q - 1)
                        w = slice(q * P, (q + 1) * P)
                        three(big[:, q % 2, :], w1h[:, w], w1l[:, w], hoff).then_inc(G_("hid_done"), 1)
                    if e == 0 and not n_is(n, 0):
                        expert_out(N - 1, E - 1)
                    if e == 1:
                        for i in range(TPK):
                            ins = pe.transpose(s1[:, 1, i * E:(i + 1) * E], lgT[:, i * P:(i + 1) * P],
                                               ident[0:E, 0:E])
                        ins.then_inc(G_("lg_done"), 1)
                    if e > 0:
                        expert_out(N, e - 1)
                    if e == 6 and not last:
                        pe.wait_ge(G_("ht_ready"), ln_count(2 * f + 1, n))
                        ln_transpose(2 * f + 1, n + 1)

            def experts(f):
                if f == 0:
                    pe.wait_ge(G_("rw_split"), 2)
                    pe.wait_ge(G_("w1_split"), 2)
                    pe.wait_ge(G_("w2_loaded"), 16)
                ln_transpose(2 * f + 1, 0)
                experts_block(f, 0, False)
                with pe.Fori(1, NBLK - 1) as n:
                    experts_block(f, n, False)
                experts_block(f, NBLK - 1, True)
                expert_out(NBLK * f + NBLK - 1, E - 1)

            experts(0)

            def project(count, task, g, b):
                wh, wl = ((wqh, wql), (wkh, wkl))[task // 2]
                three(misc[:], wh[:, g, :], wl[:, g, :], (b % 2) * 2 * BLK + (task % 2) * BLK
                      ).then_inc(G_("qkp_done"), 1)

            def values(r):
                for i in range(TPK):
                    ins = pe.matmul(misc[:, i * P:(i + 1) * P], hf[:, r, i * P:(i + 1) * P], wvT[:],
                                    start=True, stop=True)
                ins.then_inc(G_("v_done"), 1)

            def first_pass(count, g, kk, i):
                t, j = kk // 2, 2 * (kk % 2) + i
                if not (isinstance(count, int) and count == 0 and kk == 0):
                    pe.wait_ge(G_("max_done"), count + 2 * kk + i - 1)
                for th in range(2):
                    ins = pe.matmul(sm[:, i, th * BLK:(th + 1) * BLK], Q[:, g, t * P:(t + 1) * P],
                                    Km[:, g, j, th * BLK:(th + 1) * BLK], start=True, stop=True)
                ins.then_inc(G_("s1_done"), 1)

            def turn_maxima(count, half):
                pe.wait_ge(G_("mx_ready"), count + half + 1)
                for i in range(TPK):
                    ins = pe.transpose(misc[:, i * P:(i + 1) * P], MX[:, i, :], ident)
                ins.then_inc(G_("mxt_done"), 1)

            def turn_output(b, i):
                pe.wait_ge(G_("acc_stored"), 8 * b + i + 1)
                for t in range(TPK):
                    ins = pe.transpose(misc[:, t * P:(t + 1) * P], accS[:, t * P:(t + 1) * P], ident)
                ins.then_inc(G_("ot_done"), 1)

            def group_ready(done, g):
                pe.wait_ge(G_("qk_split"), 4 * done + 4)
                pe.wait_ge(G_("km_stored"), 128 * done + 128)

            pe.wait_ge(G_("wqk_split"), 4)
            ln_transpose(2, 0)
            pe.wait_ge(G_("ht_ready"), ln_count(2, 0))
            ln_transpose(2, 1)
            pe.wait_ge(G_("hlo_ready"), NBLK + 2)
            pe.wait_ge(G_("ht_ready"), ln_count(2, 1))
            for t in range(4):
                if t:
                    pe.wait_ge(G_("qkp_taken"), t)
                project(0, t, 0, 0)
            pe.wait_ge(G_("qkp_taken"), 4)
            values(0)
            pe.wait_ge(G_("v_stored"), 1)
            values(1)
            pe.wait_ge(G_("v_stored"), 2)
            for t in range(4):
                if t:
                    pe.wait_ge(G_("qkp_taken"), 4 + t)
                project(4, t, 1, 0)
            group_ready(0, 0)
            for kk in range(STEPS):
                for i in range(2):
                    first_pass(0, 0, kk, i)
                if kk == 9:
                    pe.wait_ge(G_("qkp_taken"), 8)
                    turn_maxima(0, 0)
            pe.wait_ge(G_("q_shifted"), 1)

            def output_transpose(b, r):
                for t in range(TPK):
                    ins = pe.transpose(misc[:, t * P:(t + 1) * P], ob[:, TPK * r + t, :], ident)
                ins.then_inc(G_("obt_done"), 1)

            def output_times_wo(b, r):
                if r == 0:
                    pe.wait_ge(G_("obt_stored"), 2 * b + 2)
                for t in range(TPK):
                    c = (TPK * r + t) * P
                    ins = pe.matmul(misc[:, t * P:(t + 1) * P], oT2[:, c:c + P], woT[:], start=True, stop=True)
                ins.then_inc(G_("wo_done"), 1)

            def attention_batch(b, first, last):
                prev = None if first else (G_("o_normed"), 8 * b - 1)
                for k in range(BSTEPS):
                    g, kk = divmod(k, STEPS)
                    Gn = 4 * b + g
                    more = not (last and g == 3)
                    u, t = divmod(kk, TPB)

                    def second_pass(j):
                        if not (first and k == 0 and j < 2):
                            pe.wait_ge(G_("exp_done"), HG * (BSTEPS * b + k) + j - 1)
                        pe.matmul(se[:, j % 2, :], Km[:, g, j, t * P:(t + 1) * P],
                                  Q[:, g, u * BLK:(u + 1) * BLK], start=True, stop=True
                                  ).then_inc(G_("s2_done"), 1)

                    if kk == 0:
                        pe.wait_ge(G_("q_shifted"), 2 * Gn + 1)
                        if more:
                            group_ready(Gn + 1, (g + 1) % NG)
                    if kk == 8:
                        pe.wait_ge(G_("q_shifted"), 2 * Gn + 2)
                    second_pass(0)
                    second_pass(1)
                    if k > 0:
                        times_values(b, k - 1, first)
                    elif not first:
                        times_values(b - 1, BSTEPS - 1)
                    second_pass(2)
                    second_pass(3)
                    task = None
                    if kk == 2:
                        task = (turn_maxima, (2 * Gn, 1), "q_shifted", 2 * Gn + 2)
                    if kk == 3 and g > 0:
                        task = (turn_output, (b, 2 * g - 1), "o_normed", 8 * b + 2 * g)
                    if not first and k == 1:
                        task = (turn_output, (b - 1, 7), "o_normed", 8 * b)
                    if not first and k in (3, 8):
                        task = (output_transpose, (b - 1, k // 8), "obt_stored", 2 * b - 1 + k // 8)
                    if not first and k in (9, 10):
                        task = (output_times_wo, (b - 1, k - 9), "x_added", 2 * b + k - 10)
                    if kk in (4, 5, 6, 7) and not (last and g >= 2):
                        if g == 2 and kk == 4:
                            pe.wait_ge(G_("hlo_ready"), NBLK + 2 * b + 4)
                        task = (project, (0, kk - 4, (g + 2) % NG, b + g // 2), "qkp_taken", 4 * (Gn + 2) + kk - 3)
                    if kk in (9, 10) and g == 3 and not last:
                        task = (values, (kk - 9,), "v_stored", 2 * b + 3 + kk - 9)
                    if kk == 11 and more:
                        task = (turn_maxima, (2 * (Gn + 1), 0), "q_shifted", 2 * (Gn + 1) + 1)
                    if kk == 14 and g < 2 and not last:
                        task = (ln_transpose, (2, 2 * b + 2 + g), "ht_ready", ln_count(2, 2 * b + 2 + g))
                    if kk == 12:
                        task = (turn_output, (b, 2 * g), "o_normed", 8 * b + 2 * g + 1)
                    if task:
                        if prev is not None:
                            pe.wait_ge(*prev)
                        task[0](*task[1])
                        prev = (G_(task[2]), task[3])
                    if more:
                        first_pass(2 * STEPS * (Gn + 1), (g + 1) % NG, kk, 0)
                        first_pass(2 * STEPS * (Gn + 1), (g + 1) % NG, kk, 1)

            def times_values(b, k, first=False):
                g, kk = divmod(k, STEPS)
                t = kk % TPB
                pe.wait_ge(G_("exp_done"), HG * (BSTEPS * b + k + 1))
                if kk == 0:
                    pe.wait_ge(G_("vg_ready"), 4 * b + g + 1)
                if t == 0 and not (first and k == 0):
                    pe.wait_ge(G_("acc_stored"), 8 * b + k // 8)
                for j in range(HG):
                    ins = pe.matmul(acc[RB * j:RB * (j + 1), :], Vg[:, g % 2, t, j, :], PB[:, k % 2, j, :],
                                    start=(t == 0), stop=(t == TPB - 1))
                ins.then_inc(G_("pv_done"), 1)

            attention_batch(0, True, False)
            with pe.Fori(1, B - 1) as b:
                attention_batch(b, False, False)
            attention_batch(B - 1, False, True)
            times_values(B - 1, BSTEPS - 1)
            pe.wait_ge(G_("o_normed"), 8 * B - 1)
            turn_output(B - 1, 7)
            pe.wait_ge(G_("o_normed"), 8 * B)
            output_transpose(B - 1, 0)
            pe.wait_ge(G_("obt_stored"), 2 * B - 1)
            output_transpose(B - 1, 1)
            output_times_wo(B - 1, 0)
            pe.wait_ge(G_("x_added"), 2 * B - 1)
            output_times_wo(B - 1, 1)
            pe.wait_ge(G_("x_added"), 2 * B)
            experts(1)


def kernel(**inputs):
    import numpy as np
    import concourse.bacc as bacc
    from concourse.bass_utils import run_bass_kernel_spmd

    g = {k: np.asarray(v) for k, v in inputs.items()}
    pa, pb, pf = "L0_attn_a_", "L0_attn_b_", "L0_ffn_"
    r, c = np.triu_indices(OD, k=1)

    wom = np.zeros((D, OD * OD), np.float32)
    wom[:, r * OD + c] = g[pa + "omega_proj_w"].T
    bom = np.zeros((1, OD * OD), np.float32)
    bom[0, r * OD + c] = g[pa + "omega_proj_b"]

    def stacked(w):
        o = np.zeros((D, NG, HG, RB), np.float32)
        t = w.reshape(NG, HG, DH, D).transpose(3, 0, 1, 2)
        for k in range(3):
            o[:, :, :, k * DH:(k + 1) * DH] = t
        return o.reshape(D, NG * P)

    def stacked_bias(v, one):
        o = np.zeros((NG, HG, RB), np.float32)
        for k in range(3):
            o[:, :, k * DH:(k + 1) * DH] = v.reshape(NG, HG, DH)
        o[:, :, 3 * DH:3 * DH + 2] = one
        return o.reshape(NG, P).T

    cst = np.zeros((P, C_END), np.float32)
    cst[:, :P] = np.eye(P)
    rows = np.arange(P) % RB
    cst[:, C_NMQ] = np.where((rows >= 2 * DH) & (rows < 3 * DH), -1.0, 0.0)
    cst[:, C_NMK] = np.where((rows >= DH) & (rows < 2 * DH), -1.0, 0.0)
    cst[:, C_IOTA:C_ONE] = np.arange(VC)
    cst[:, C_ONE] = 1.0

    arrays = {
        "x": g[pa + "x"], "cst": cst, "w_om": wom, "b_om": bom,
        "woutT": g[pa + "omega_out_w"].T, "bout": g[pa + "omega_out_b"].reshape(1, D),
        "wpiT": g[pa + "vq_proj_in_w"].T, "bpi": g[pa + "vq_proj_in_b"].reshape(1, VD),
        "wpoT": g[pa + "vq_proj_out_w"].T, "bpo": g[pa + "vq_proj_out_b"].reshape(1, D),
        "cb": g[pa + "codebook"], "mix": g[pa + "omega_mix"].reshape(1, 1),
        "vqm": g[pa + "vq_mix"].reshape(1, 1), "nw": g[pa + "norm_w"].reshape(1, D),
        "wqs": stacked(g[pb + "Wq"]), "wks": stacked(g[pb + "Wk"]),
        "bqs": stacked_bias(g[pb + "bq"], 0.0), "bks": stacked_bias(g[pb + "bk"], 1.0),
        "wvT": g[pb + "Wv"].reshape(H * DH, D).T, "bv": g[pb + "bv"].reshape(1, H * DH),
        "woT": g[pb + "Wo"].T, "bo": g[pb + "bo"].reshape(1, D),
        "rwT": g[pf + "router_w"].T, "w1": g[pf + "w1"], "w2": g[pf + "w2"],
    }
    nc = bacc.Bacc("TRN2", target_bir_lowering=False, num_devices=1)
    feeds, aps = {}, {}
    for name, v in arrays.items():
        v = np.ascontiguousarray(v)
        feeds[f"in_{name}"] = v
        aps[name] = nc.dram_tensor(f"in_{name}", v.shape, mybir.dt.from_np(v.dtype), kind="ExternalInput").ap()
    res = nc.dram_tensor("out_0", (B, L, D), F32, kind="ExternalOutput").ap()
    hybrid_layer(nc, aps, res)
    done = run_bass_kernel_spmd(nc, [feeds], core_ids=[0])
    return done.results[0]["out_0"]
```

```python
from contextlib import ExitStack

import concourse.bass as bass
from concourse import mybir

ALU = mybir.AluOpType
ACT = mybir.ActivationFunctionType
AX = mybir.AxisListType
F32 = mybir.dt.float32
F32R = mybir.dt.float32r
I32 = mybir.dt.int32
U32 = mybir.dt.uint32

P = 128
B, L, D = 4, 1024, 128
TPB = L // P
BLK = 512
NBLK = B * L // BLK
TPK = BLK // P
LNA = 4
RMS_GROUPS = ((0, 2), (2, 2), (4, 4))
OD = 64
VD, VC = 64, 32
E, HID = 8, 256
CH = HID // P
H, DH = 16, 8
HG = 4
NG = H // HG
RB = 32
STEPS = 2 * TPB
BSTEPS = NG * STEPS
LN_EPS, RMS_EPS, NORM_EPS = 1e-5, 1e-6, 1e-12
RSQRT_MAGIC = 1597463007.0
OMEGA_HALF = OD * OD // 2

C_ID, C_NMQ, C_NMK, C_IOTA, C_ONE, C_END = 0, 128, 129, 130, 162, 163


def ds(start, n):
    return bass.ds(start, n)


class Chain:

    def __init__(self, eng, sem):
        self.eng, self.sem, self.n, self.base = eng, sem, 0, 0

    def __call__(self, ins):
        self.n += 1
        ins.then_inc(self.sem, 1)
        self.eng.wait_ge(self.sem, self.base + self.n)

    def enter(self, rounds_done, per_round):
        self.base, self.n0 = rounds_done * per_round, self.n

    def leave(self, rounds, per_round):
        assert self.n - self.n0 == per_round, (self.n - self.n0, per_round)
        self.base, self.n = 0, self.n0 + rounds * per_round


FFN_CHAIN = 23
ATT_CHAIN = 44


def hybrid_layer(nc, a, out):
    ctx = ExitStack()
    with ctx:
        def sb(name, shape, dt=F32):
            return ctx.enter_context(nc.sbuf_tensor(name, shape, dt))

        def ps(name, shape, dt=F32):
            return ctx.enter_context(nc.psum_tensor(name, shape, dt))

        def sem(name):
            return ctx.enter_context(nc.semaphore(name))

        x = sb("x", [P, B * TPB * D])
        hTh = sb("hTh", [P, 4 * BLK], F32R)
        hTl = sb("hTl", [P, 4 * BLK], F32R)
        w1h = sb("w1h", [P, E * HID], F32R)
        w1l = sb("w1l", [P, E * HID], F32R)
        w2s = sb("w2s", [P, E * CH, D])
        Km = sb("Km", [P, NG, HG, L], F32R)
        Q = sb("Q", [P, NG, L], F32R)
        PB = sb("PB", [P, 2, HG, BLK])
        SC = sb("SC", [P, 4096])
        VH = sb("VH", [P, 2048])
        Vg = sb("Vg", [P, 2, TPB, HG, RB])
        Kst = sb("Kst", [P, BLK], F32R)
        tr = sb("tr", [P, BLK], F32R)
        wqh = sb("wqh", [P, NG, P], F32R)
        wql = sb("wql", [P, NG, P], F32R)
        wkh = sb("wkh", [P, NG, P], F32R)
        wkl = sb("wkl", [P, NG, P], F32R)
        wvT = sb("wvT", [P, H * DH])
        woT = sb("woT", [P, D])
        rwf = sb("rwf", [P, E])
        rwh = sb("rwh", [P, E], F32R)
        rwl = sb("rwl", [P, E], F32R)
        cst = sb("cst", [P, C_END])
        bqk = sb("bqk", [P, 2 * NG])
        nwb = sb("nwb", [P, D])
        cbb = sb("cbb", [P, D])
        small = sb("small", [P, 64])
        ones = sb("ones", [P, P])
        wexp = sb("wexp", [P, TPK * E])
        hb = sb("hb", [P, TPK, D])

        ident = cst[:, C_ID:C_ID + P]
        nmq, nmk = cst[:, C_NMQ:C_NMQ + 1], cst[:, C_NMK:C_NMK + 1]
        iota = cst[:, C_IOTA:C_ONE]
        one = cst[:, C_ONE:C_END].rearrange("p (a b c) -> p a b c", a=1, b=1)
        relu_b, sq_b = PB[:, 0], PB[:, 1]
        hTa = PB[:].rearrange("p a j n -> p (a j n)")
        w_om = SC[:]
        ob = SC[:, 0:1024].rearrange("p (t c) -> p t c", c=P)
        oT2 = SC[:, 1024:2048]
        MX = SC[:, 2048:2560].rearrange("p (t c) -> p t c", c=P)
        accS = SC[:, 2560:3072]
        qf = SC[:, 3072:4096].rearrange("p (u n) -> p u n", u=2)
        tA = SC[:, 0:1024].rearrange("p (u n) -> p u n", u=2)
        sqA = SC[:, 1024:1536]
        w2f = w2s[:].rearrange("p k d -> p (k d)")
        hbA = w2f.rearrange("p (r t d) -> p r t d", r=LNA, d=D)
        par_buf = (VH[:], w2f)
        Vst = VH[:, 0:1024]
        hf = VH[:, 1024:2048].rearrange("p (u n) -> p u n", u=2)
        w1f = VH[:]
        wqf = Vg[:].rearrange("p a t j r -> p (a t j r)")[:, 0:2 * NG * P]

        st = sb("st", [P, LNA * TPK, 6])
        mv = sb("mv", [P, LNA * TPK, 2])
        ve = sb("ve", [P, LNA * TPK])
        rs = sb("rs", [P, LNA * TPK])
        nt = sb("nt", [P, LNA * TPK])
        ssq = sb("ssq", [P, NBLK * TPK])
        hsum = sb("hsum", [P, NBLK])
        hm = sb("hm", [P, B])
        lgT = sb("lgT", [E, BLK])
        lg = sb("lg", [P, TPK, E])
        m8 = sb("m8", [P, TPK, 8])
        ix = sb("ix", [P, TPK, 8], U32)
        ixf = sb("ixf", [P, TPK, 2])
        dd = sb("dd", [P, TPK])
        ed = sb("ed", [P, TPK])
        eds = sb("eds", [P, TPK])
        pr = sb("pr", [P, 2, TPK])
        wa = sb("wa", [P, TPK, E])
        wb = sb("wb", [P, TPK, E])
        mxp = sb("mxp", [P, TPB, HG])
        rc = sb("rc", [P, TPK, HG])
        vgf = Vg[:].rearrange("p a t j r -> p (a t j r)")
        Ub = vgf[0:OD, 1024:1280].rearrange("p (b j) -> p b j", b=B)
        Nn = SC[0:OD, 1024:1280].rearrange("p (b j) -> p b j", b=B)
        Wout = vgf[0:OD, 1280:1408]
        Wouth = vgf[0:OD, 1408:1536]
        Mg = SC[:, 1536:2048].rearrange("p (b d) -> p b d", b=B)
        wpi = vgf[:, 1536:1600]
        wpo = vgf[0:VD, 1600:1728]
        code = vgf[0:VC, 1728:1792]
        coden = vgf[0:VC, 1792:1856]
        bpb = vgf[0:B, 1856:1920]
        crow = SC[:, 2048:2560].rearrange("p (b d) -> p b d", b=B)
        row = lgT[0:1, :].rearrange("p (k d) -> p k d", k=4)
        cbrow = vgf[0:1, 1920:2048]
        bpc = sb("bpc", [VD, 1])
        v4 = sb("v4", [B, VD])
        v4n = sb("v4n", [B, VD])
        vT = sb("vT", [VD, B])
        vqT = sb("vqT", [VD, B])
        vnT = sb("vnT", [VD, B])
        cnT = sb("cnT", [VD, VC])
        ssn = sb("ssn", [VC, 2])
        rsn = sb("rsn", [VC, 2])
        ntn = sb("ntn", [VC, 2])
        sc4 = sb("sc4", [B, VC])
        m84 = sb("m84", [B, 8])
        ix4 = sb("ix4", [B, 8], U32)
        if4 = sb("if4", [B, 1])
        oh = sb("oh", [B, VC])
        ohT = sb("ohT", [VC, B])
        pad = sb("pad", [1, 1])
        bvc = sb("bvc", [P, 1])
        mix = small[:, 0:1]
        vqm = small[:, 1:2]

        six = ps("six", [P, 6, BLK])
        big, s1 = six[:, 0:4], six[:, 4:6]
        se = six[:, 0:2]
        sl = six[:, 0:HG]
        sm = six[:, 2:6].rearrange("p (r a) n -> p r (a n)", a=2)
        acc = ps("acc", [P, BLK])
        misc = ps("misc", [P, BLK])

        S = {n: sem(n) for n in (
            "x0_loaded", "x1_loaded", "x2_loaded", "x3_loaded", "cst_loaded", "w1_loaded", "w2_loaded",
            "wom_loaded", "vq_loaded", "attw_loaded", "wqk_loaded", "ub_loaded", "bu0_loaded", "bu1_loaded",
            "dve_step", "h_ready", "lnt_done", "ht_ready", "hlo_ready",
            "w1_split", "rw_split", "wqk_split", "km_zeroed", "pool_zeroed", "fills_done",
            "hm_ready", "vqp_done", "par_done", "par_taken", "ubt_done", "nn_ready", "om_done", "om_taken",
            "cn_ready", "cnt_done", "cnt_taken", "vsc_done", "oh_ready", "oht_done", "oht_taken", "code_done",
            "vq_ready", "crow_done", "crow_ready", "mg_ready", "cb_ready", "cbr_done", "cbr_taken", "cbb_done",
            "cbb_ready", "a2_done", "a2_sq", "t_ready", "x1_ready",
            "router_done", "lgt_stored", "lg_done", "lg_taken", "d_ready", "ed_ready",
            "hid_done", "relu_done", "sqv_done", "sqa_done", "y_done", "comb_done",
            "s2_done", "s1_done", "pv_done", "exp_done", "max_done", "acc_stored",
            "qkp_done", "qkp_taken", "qk_split", "km_stored", "mx_ready", "mxt_done", "q_shifted",
            "ot_done", "o_normed", "obt_done", "obt_stored", "wo_done", "x_added", "x_biased",
            "v_done", "v_stored", "vg_ready", "out_stored", "mx_zeroed")}
        G_ = S.__getitem__
        x_loaded = [G_(f"x{b}_loaded") for b in range(B)]

        block = ctx.enter_context(nc.Block())

        def ln_count(kind, n):
            return NBLK * kind + n + 1

        def bank_a1(n):
            return misc[:] if n % 2 == 0 else acc[:]

        def bank_a2(n):
            return six[:, n, :] if n < 6 else acc[:] if n == 6 else six[:, 3, :]

        @block.sync
        def _(sp):
            xv = a["x"].rearrange("b (p i) d -> p b (i d)", p=P)
            for b in range(B):
                sp.dma_start(x[:, b * L:(b + 1) * L], xv[:, b, :]).then_inc(x_loaded[b], 16)
                if b == 0:
                    sp.dma_start(cst[:], a["cst"]).then_inc(G_("cst_loaded"), 16)
            sp.dma_start(w1f.rearrange("p (e h) -> p e h", e=E),
                         a["w1"].rearrange("e d h -> d e h")).then_inc(G_("w1_loaded"), 16)
            sp.dma_start(w_om, a["w_om"]).then_inc(G_("wom_loaded"), 16)
            for dst, src in ((Wout, a["woutT"]), (wpi, a["wpiT"]), (wpo, a["wpoT"]), (code, a["cb"]),
                             (row[0:1, 0, :], a["bpo"]), (row[0:1, 1, :], a["bout"]), (row[0:1, 2, :], a["bo"]),
                             (bpc[:], a["bpi"].rearrange("a n -> n a")), (bpb, a["bpi"].broadcast_to([B, VD])),
                             (mix, a["mix"].broadcast_to([P, 1])), (vqm, a["vqm"].broadcast_to([P, 1])),
                             (nwb[:], a["nw"].broadcast_to([P, D])), (bvc[:], a["bv"].rearrange("a n -> n a"))):
                sp.dma_start(dst, src).then_inc(G_("vq_loaded"), 16)
            for dst, src in ((wqf[:, 0:NG * P], a["wqs"]), (wqf[:, NG * P:2 * NG * P], a["wks"]),
                             (rwf[:], a["rwT"])):
                sp.dma_start(dst, src).then_inc(G_("wqk_loaded"), 16)
            for dst, src in ((wvT[:], a["wvT"]), (woT[:], a["woT"]), (bqk[:, 0:NG], a["bqs"]),
                             (bqk[:, NG:2 * NG], a["bks"])):
                sp.dma_start(dst, src).then_inc(G_("attw_loaded"), 16)
            for hv in range(2):
                if hv == 0:
                    sp.wait_ge(G_("w1_split"), 2)
                else:
                    sp.wait_ge(G_("lnt_done"), NBLK)
                sp.dma_start(par_buf[hv][32:32 + B, :], a["b_om"][:, hv * OMEGA_HALF:(hv + 1) * OMEGA_HALF]
                             .broadcast_to([B, OMEGA_HALF])).then_inc(G_(f"bu{hv}_loaded"), 16)
            for hv in range(2):
                sp.wait_ge(G_("par_taken"), 4 * (hv + 1))
                for b in range(B):
                    sp.dma_start(Ub[hv * 32:(hv + 1) * 32, b, :],
                                 par_buf[hv][b:b + 1, :].rearrange("o (i j) -> o i j", j=OD)
                                 ).then_inc(G_("ub_loaded"), 16)
            sp.wait_ge(G_("ub_loaded"), 32 * B)
            sp.dma_start(w2s[:], a["w2"].rearrange("e (c h) d -> h (e c) d", c=CH)).then_inc(G_("w2_loaded"), 16)

            def spread_keys(done, g):
                for half in range(2):
                    sp.wait_ge(G_("qk_split"), 4 * done + 2 * half + 1)
                    for j in range(HG):
                        sp.dma_start(Km[RB * j:RB * (j + 1), g, j, half * BLK:(half + 1) * BLK].bitcast(F32),
                                     Kst[RB * j:RB * (j + 1), :].bitcast(F32)).then_inc(G_("km_stored"), 16)

            sp.wait_ge(G_("km_zeroed"), 1)
            spread_keys(0, 0)
            spread_keys(1, 1)
            with sp.Fori(0, B - 1) as b:
                for g in range(NG):
                    spread_keys(4 * b + g + 2, (g + 2) % NG)
            spread_keys(4 * (B - 1) + 2, 2)
            spread_keys(4 * (B - 1) + 3, 3)

            ov = out.rearrange("b (p u i) d -> p b u (i d)", p=P, u=2)
            with sp.Fori(0, B) as b:
                for u in range(2):
                    sp.wait_ge(G_("comb_done"), E * (NBLK + 2 * b + u + 1))
                    sp.dma_start(ov[:, ds(b, 1), u, :], x[:, ds(b * L + u * BLK, BLK)]
                                 .rearrange("p (o n) -> p o n", o=1)).then_inc(G_("out_stored"), 16)
            sp.wait_ge(G_("out_stored"), 16 * NBLK)

        @block.gpsimd
        def _(pl):
            pl.memset(ones[:], 1.0).then_inc(G_("fills_done"), 1)
            pl.wait_ge(G_("cst_loaded"), 16)
            pl.wait_ge(G_("w1_loaded"), 16)
            pl.tensor_copy(w1h[:], w1f).then_inc(G_("w1_split"), 1)
            pl.wait_ge(G_("w1_split"), 1)
            pl.tensor_tensor(w1l[:], w1f, w1h[:].bitcast(F32), ALU.subtract).then_inc(G_("w1_split"), 1)
            pl.wait_ge(G_("wqk_loaded"), 48)
            pl.tensor_copy(rwh[:], rwf[:]).then_inc(G_("rw_split"), 1)
            pl.wait_ge(G_("rw_split"), 1)
            pl.tensor_tensor(rwl[:], rwf[:], rwh[:].bitcast(F32), ALU.subtract).then_inc(G_("rw_split"), 1)

            for g in range(NG):
                ins = pl.memset(Km[:, g].bitcast(F32), 0.0)
            ins.then_inc(G_("km_zeroed"), 1)

            def residual_add(n):
                pl.wait_ge(G_("t_ready"), n + 1)
                pl.tensor_tensor(x[:, n * BLK:(n + 1) * BLK], x[:, n * BLK:(n + 1) * BLK], tA[:, n % 2, :],
                                 ALU.add).then_inc(G_("x1_ready"), 1)

            def low_part(kind, n):
                m = NBLK * (kind - 1) + n + 1
                pl.wait_ge(G_("ht_ready"), ln_count(kind, n))
                pl.tensor_tensor(hTl[:, ds((n % 4) * BLK, BLK)], hf_block(n), hTh[:, ds((n % 4) * BLK, BLK)]
                                 .bitcast(F32), ALU.subtract).then_inc(G_("hlo_ready"), 1)
                return m

            def hf_block(n):
                return VH[:, ds(1024 + (n % 2) * BLK, BLK)]

            for n in range(NBLK):
                residual_add(n)
                if n == RMS_GROUPS[-1][0] - 1:
                    low_part(1, 0)
            low_part(1, 1)
            wq4 = wqf.rearrange("p (a g c) -> p a g c", a=2, g=NG)
            for s, (hi, lo) in enumerate(((wqh, wql), (wkh, wkl))):
                pl.tensor_copy(hi[:], wq4[:, s]).then_inc(G_("wqk_split"), 1)
                pl.wait_ge(G_("wqk_split"), 2 * s + 1)
                pl.tensor_tensor(lo[:], wq4[:, s], hi[:].bitcast(F32), ALU.subtract).then_inc(G_("wqk_split"), 1)
            pl.wait_ge(G_("wqk_split"), 4)
            pl.memset(Vg[:], 0.0).then_inc(G_("pool_zeroed"), 1)
            pl.memset(MX, 0.0).then_inc(G_("mx_zeroed"), 1)
            pl.wait_ge(G_("pool_zeroed"), 1)
            pl.memset(Vg[:, :, :, :, DH:DH + 1], 1.0).then_inc(G_("pool_zeroed"), 1)
            with pl.Fori(2, NBLK) as n:
                low_part(1, n)

            def bias_block(n):
                pl.wait_ge(G_("h_ready"), ln_count(2, n))
                xb = x[:, ds(n * BLK, BLK)].rearrange("p (t c) -> p t c", c=D)
                pl.tensor_tensor(xb, xb, cbb[:].rearrange("p (o c) -> p o c", o=1).broadcast_to([P, TPK, D]),
                                 ALU.add).then_inc(G_("x_biased"), 1)

            def group_values(g):
                v = Vst.rearrange("p (t h d) -> p t h d", t=TPB, d=DH)[:, :, HG * g:HG * (g + 1), :]
                pl.tensor_tensor(Vg[:, g % 2, :, :, 0:DH], v, one.broadcast_to([P, TPB, HG, DH]), ALU.mult).then_inc(G_("vg_ready"), 1)

            low_part(2, 0)
            low_part(2, 1)
            pl.wait_ge(G_("v_stored"), 2)
            pl.wait_ge(G_("pool_zeroed"), 2)
            group_values(0)
            pl.wait_ge(G_("cbb_ready"), 1)
            bias_block(0)
            bias_block(1)

            def attention_batch(b, last):
                group_values(1)
                if not last:
                    for u in range(2):
                        low_part(2, 2 * b + 2 + u)
                        bias_block(2 * b + 2 + u)
                for g in (2, 3):
                    pl.wait_ge(G_("pv_done"), BSTEPS * b + STEPS * (g - 1))
                    group_values(g)
                if not last:
                    pl.wait_ge(G_("v_stored"), 2 * b + 4)
                    pl.wait_ge(G_("pv_done"), BSTEPS * b + STEPS * 3)
                    group_values(0)
                if not last:
                    pl.wait_ge(G_("pv_done"), BSTEPS * b + BSTEPS)

            with pl.Fori(0, B - 1) as b:
                attention_batch(b, False)
            attention_batch(B - 1, True)

            low_part(3, 0)
            with pl.Fori(1, NBLK) as n:
                low_part(3, n)

        @block.scalar
        def _(act):
            def ht_out(kind, n, guard=None):
                act.wait_ge(G_("lnt_done"), ln_count(kind, n))
                if guard is not None:
                    act.wait_ge(*guard)
                act.activation(VH[:, ds(1024 + (n % 2) * BLK, BLK)], misc[:], ACT.Copy)
                act.activation(hTh[:, ds((n % 4) * BLK, BLK)], misc[:], ACT.Copy).then_inc(G_("ht_ready"), 1)

            for n in range(NBLK):
                act.wait_ge(G_("lnt_done"), ln_count(0, n))
                act.activation(hTa[:, n * BLK:(n + 1) * BLK], bank_a1(n), ACT.Copy,
                               accum_out=hsum[:, n:n + 1]).then_inc(G_("ht_ready"), 1)
            for n in range(NBLK):
                act.wait_ge(G_("a2_done"), n + 1)
                if n:
                    act.wait_ge(G_("a2_sq"), n)
                for i in range(TPK):
                    ins = act.activation(sqA[:, i * D:(i + 1) * D], bank_a2(n)[:, i * P:(i + 1) * P], ACT.Square,
                                         accum_out=ssq[:, n * TPK + i:n * TPK + i + 1])
                ins.then_inc(G_("a2_sq"), 1)
            act.wait_ge(G_("ub_loaded"), 32 * B)
            ht_out(1, 0)

            def lo_free(kind, n):
                return G_("hlo_ready"), NBLK * (kind - 1) + n - 1

            def experts_block(f, n, last, beside=None):
                N = NBLK * f + n
                act.wait_ge(G_("router_done"), N + 1)
                act.activation(lgT[:], s1[0:E, 0, :], ACT.Copy).then_inc(G_("lgt_stored"), 1)
                for e in range(E):
                    for c in range(CH):
                        q = CH * e + c
                        act.wait_ge(G_("hid_done"), CH * E * N + q + 1)
                        if c == 0 and not (f == 0 and n_is(n, 0) and e < 2):
                            act.wait_ge(G_("sqv_done"), E * N + e - 1)
                        act.activation(relu_b[:, q % 4, :], big[:, q % 2, :], ACT.Relu
                                       ).then_inc(G_("relu_done"), 1)
                    act.wait_ge(G_("relu_done"), CH * E * N + CH * e + 2)
                    if not (f == 0 and n_is(n, 0) and e < 2):
                        act.wait_ge(G_("y_done"), E * N + e - 1)
                    act.activation(sq_b[:, 2 * (e % 2) + 1, :], relu_b[:, (CH * e + 1) % 4, :], ACT.Square
                                   ).then_inc(G_("sqa_done"), 1)
                    if e == 1:
                        act.wait_ge(G_("d_ready"), N + 1)
                        act.activation(ed[:], dd[:], ACT.Exp).then_inc(G_("ed_ready"), 1)
                    if e == 6 and not last:
                        ht_out(2 * f + 1, n + 1, lo_free(2 * f + 1, n + 1))
                    if beside:
                        beside(e)

            def n_is(n, v):
                return isinstance(n, int) and n == v

            def experts(f):
                experts_block(f, 0, False, attention_end if f else None)
                with act.Fori(1, NBLK - 1) as n:
                    experts_block(f, n, False)
                experts_block(f, NBLK - 1, True, None if f else attention_start)

            def attention_start(e):
                if e == 0:
                    act.wait_ge(G_("attw_loaded"), 64)
                    act.activation(bqs, bqk[:, 0:NG], ACT.Copy, scale=DH ** -0.5).then_inc(G_("cb_ready"), 1)
                    act.wait_ge(G_("cb_ready"), 1)
                elif e in (1, 5):
                    ht_out(2, e // 5)
                elif e in (3, 4, 7):
                    proj_out(0, {3: 0, 4: 1, 7: 2}[e], 0)

            def attention_end(e):
                if e in (2, 3):
                    output_rows(B - 1, e - 2)

            def proj_out(count, task, g):
                act.wait_ge(G_("qkp_done"), count + task + 1)
                if not (isinstance(count, int) and count + task < 1):
                    act.wait_ge(G_("qk_split"), count + task)
                bias = bqs[:, g:g + 1] if task % 2 else bqk[:, NG + g:NG + g + 1]
                scale = DH ** -0.5 if task % 2 else 1.0
                act.activation(qf[:, task % 2, :], misc[:], ACT.Identity, bias=bias, scale=scale)
                act.activation(tr[:], misc[:], ACT.Identity, bias=bias, scale=scale
                               ).then_inc(G_("qkp_taken"), 1)

            def v_out(count, r):
                act.wait_ge(G_("v_done"), count + r + 1)
                act.activation(Vst[:, r * BLK:(r + 1) * BLK], misc[:], ACT.Copy).then_inc(G_("v_stored"), 1)

            bqs = small[:, 8:8 + NG]
            experts(0)
            proj_out(0, 3, 0)
            for r in range(2):
                v_out(0, r)
            for t in range(4):
                proj_out(4, t, 1)

            def output_rows(b, r):
                act.wait_ge(G_("obt_done"), 2 * b + r + 1)
                act.activation(oT2[:, r * BLK:(r + 1) * BLK], misc[:], ACT.Copy).then_inc(G_("obt_stored"), 1)

            def attention_batch(b, first, last):
                for k in range(BSTEPS):
                    g, kk = divmod(k, STEPS)
                    for j in range(HG):
                        act.wait_ge(G_("s2_done"), HG * (BSTEPS * b + k) + j + 1)
                        if j == 0 and not (first and k < 2):
                            act.wait_ge(G_("pv_done"), BSTEPS * b + k - 1)
                        scores = sl[:, j, :] if last and g == NG - 1 else se[:, j % 2, :]
                        act.activation(PB[:, k % 2, j, :], scores, ACT.Exp).then_inc(G_("exp_done"), 1)
                    if kk in (0, 8) and k > 0:
                        acc_out(b, k // 8 - 1, first)
                    if k == 0 and not first:
                        acc_out(b - 1, 7)
                    if k in (3, 8) and not first:
                        output_rows(b - 1, k // 8)
                    if kk in (4, 5, 6, 7) and not (last and g >= 2):
                        proj_out(4 * (4 * b + g + 2), kk - 4, (g + 2) % NG)
                    if not last and g == 3 and kk in (9, 10):
                        if kk == 9:
                            act.wait_ge(G_("vg_ready"), 4 * b + 4)
                        v_out(2 * b + 2, kk - 9)
                    if not last and g in (0, 1) and kk == 14:
                        ht_out(2, 2 * b + 2 + g, (G_("hlo_ready"), NBLK + 2 * b + 1 + g))
                    if last and g == 3 and kk == 9:
                        ht_out(3, 0, (G_("v_done"), 2 * B))

            def acc_out(b, i, first=False):
                act.wait_ge(G_("pv_done"), BSTEPS * b + 8 * (i + 1))
                if not (first and i == 0):
                    act.wait_ge(G_("ot_done"), 8 * b + i)
                act.activation(accS, acc[:], ACT.Copy).then_inc(G_("acc_stored"), 1)

            attention_batch(0, True, False)
            with act.Fori(1, B - 1) as b:
                attention_batch(b, False, False)
            attention_batch(B - 1, False, True)
            acc_out(B - 1, 7)
            experts(1)

        @block.vector
        def _(dve):
            link = Chain(dve, G_("dve_step"))

            def rsqrt(v, y, t):
                yi = y.bitcast(I32)
                link(dve.tensor_scalar(yi, v.bitcast(I32), 1, None, ALU.arith_shift_right))
                link(dve.tensor_scalar(yi, yi, -1.0, RSQRT_MAGIC, ALU.mult, ALU.add))
                for _ in range(3):
                    link(dve.tensor_tensor(t, y, y, ALU.mult))
                    link(dve.scalar_tensor_tensor(out=t, in0=t, scalar=-0.5, in1=v, op0=ALU.mult, op1=ALU.mult))
                    link(dve.scalar_tensor_tensor(out=y, in0=t, scalar=1.5, in1=y, op0=ALU.add, op1=ALU.mult))

            def ln_stats(n, tiles=TPK):
                for i in range(tiles):
                    ins = dve.bn_stats(st[:, i, :], x[:, ds(n * BLK + i * D, D)])
                link(ins)
                dve.memset(pad[:], 0.0)
                for i in range(tiles):
                    ins = dve.bn_aggr(mv[:, i, :], st[:, i, :])
                link(ins)
                link(dve.tensor_scalar(ve[:, 0:tiles], mv[:, 0:tiles, 1], LN_EPS, None, ALU.add))

            def ln_rsqrt(tiles=TPK):
                rsqrt(ve[:, 0:tiles], rs[:, 0:tiles], nt[:, 0:tiles])

            def ln_apply(n, dst, k):
                for i in range(TPK):
                    c = k * TPK + i
                    ins = dve.tensor_scalar(dst[:, i, :], x[:, ds(n * BLK + i * D, D)], mv[:, c, 0:1],
                                            rs[:, c:c + 1], ALU.subtract, ALU.mult)
                ins.then_inc(G_("h_ready"), 1)

            def ln_norm(kind, n):
                if not (kind == 1 and n_is(n, 0)):
                    dve.wait_ge(G_("lnt_done"), ln_count(kind, n) - 1)
                ln_apply(n, hb, 0)

            def layer_norm(kind, n):
                ln_stats(n)
                ln_rsqrt()
                ln_norm(kind, n)

            def n_is(n, v):
                return isinstance(n, int) and n == v

            def over_b(ap):
                return ap.broadcast_to([ap.shape[0], B, D])

            for n in range(0, NBLK, LNA):
                for b in range(n // 2, (n + LNA) // 2):
                    dve.wait_ge(x_loaded[b], 16)
                ln_stats(n, LNA * TPK)
                ln_rsqrt(LNA * TPK)
                if n == LNA:
                    dve.wait_ge(G_("vq_loaded"), 13 * 16)
                    link(dve.tensor_tensor(coden, code, code, ALU.mult))
                    link(dve.memset(ssn[:], 1.0))
                    link(dve.reduce_sum(ssn[:, 0:1], coden, AX.X))
                    link(dve.tensor_scalar(row[0:1, 3, :], row[0:1, 1, :], mix[0:1, :], None, ALU.mult))
                    link(dve.tensor_scalar(Wouth, Wout, 0.5, None, ALU.mult))
                    dve.wait_ge(G_("cbr_done"), 1)
                    dve.tensor_tensor(cbrow, s1[0:1, 1, 256:256 + D], row[0:1, 2, :], ALU.add
                                      ).then_inc(G_("cbr_taken"), 1)
                for k in range(LNA):
                    if n:
                        dve.wait_ge(G_("lnt_done"), n + k - LNA + 1)
                    ln_apply(n + k, hbA[:, k], k)
            dve.wait_ge(G_("cbb_done"), 1)
            dve.tensor_copy(cbb[:], s1[:, 0, 0:D]).then_inc(G_("cbb_ready"), 1)

            dve.wait_ge(G_("ht_ready"), NBLK)
            dve.wait_ge(G_("cst_loaded"), 16)
            hs2 = hsum[:].rearrange("p (b u) -> p b u", u=2)
            link(dve.tensor_tensor(hm[:], hs2[:, :, 0], hs2[:, :, 1], ALU.add))
            dve.tensor_scalar(hm[:], hm[:], 1.0 / L, None, ALU.mult).then_inc(G_("hm_ready"), 1)

            def omega_params(c):
                dve.wait_ge(G_(f"bu{c // 4}_loaded"), 16)
                dve.wait_ge(G_("par_done"), c + 1)
                buf, cols = par_buf[c // 4], slice((c % 4) * BLK, (c % 4 + 1) * BLK)
                dve.tensor_tensor(buf[0:B, cols], big[0:B, c % 4, :], buf[32:32 + B, cols], ALU.add
                                  ).then_inc(G_("par_taken"), 1)

            dve.wait_ge(G_("vqp_done"), 1)
            link(dve.tensor_tensor(v4[:], s1[0:B, 0, 64:128], bpb, ALU.add))
            link(dve.tensor_scalar(vT[:], s1[0:VD, 0, 0:B], bpc[:, 0:1], None, ALU.add))
            link(dve.tensor_tensor(v4n[:], v4[:], v4[:], ALU.mult))
            link(dve.reduce_sum(ssn[0:B, 1:2], v4n[:], AX.X))
            rsqrt(ssn[:], rsn[:], ntn[:])
            link(dve.tensor_scalar(rsn[:], rsn[:], 1.0 / NORM_EPS, None, ALU.min))
            dve.tensor_scalar(coden, code, rsn[:, 0:1], None, ALU.mult)
            dve.tensor_scalar(v4n[:], v4[:], rsn[0:B, 1:2], None, ALU.mult).then_inc(G_("cn_ready"), 1)
            for c in range(4):
                omega_params(c)
            dve.wait_ge(G_("cnt_done"), 1)
            dve.tensor_copy(cnT[:], s1[0:VD, 1, 0:VC])
            dve.tensor_copy(vnT[:], s1[0:VD, 1, VC:VC + B]).then_inc(G_("cnt_taken"), 1)
            omega_params(4)
            omega_params(5)
            dve.wait_ge(G_("vsc_done"), 1)
            link(dve.tensor_copy(sc4[:], s1[0:B, 1, 64:64 + VC]))
            link(dve.max(m84[:], sc4[:]))
            link(dve.max_index(ix4[:], m84[:], sc4[:]))
            link(dve.tensor_copy(if4[:], ix4[:, 0:1]))
            dve.tensor_scalar(oh[:], iota[0:B, :], if4[:, 0:1], None, ALU.is_equal).then_inc(G_("oh_ready"), 1)
            omega_params(6)
            omega_params(7)
            dve.wait_ge(G_("oht_done"), 1)
            dve.tensor_copy(ohT[:], s1[0:VC, 1, 128:128 + B]).then_inc(G_("oht_taken"), 1)
            dve.wait_ge(G_("code_done"), 1)
            link(dve.tensor_tensor(vqT[:], s1[0:VD, 1, 160:160 + B], vT[:], ALU.subtract))
            dve.tensor_tensor(vqT[:], vqT[:], vT[:], ALU.add).then_inc(G_("vq_ready"), 1)
            link(dve.memset(crow, 0.0))
            dve.wait_ge(G_("crow_done"), 1)
            link(dve.tensor_tensor(crow[0:1], s1[0:1, 0, :].rearrange("p (b d) -> p b d", b=B),
                                   over_b(row[0:1, 0:1, :]), ALU.add))
            dve.scalar_tensor_tensor(out=crow[0:1], in0=crow[0:1], scalar=vqm[0:1, :], in1=over_b(row[0:1, 3:4, :]),
                                     op0=ALU.mult, op1=ALU.add).then_inc(G_("crow_ready"), 1)
            idb = ident.rearrange("p (o d) -> p o d", o=1)
            dve.tensor_copy(Mg[OD:P], over_b(idb[OD:P]))
            dve.wait_ge(G_("ubt_done"), 1)
            dve.tensor_tensor(Nn[:], misc[0:OD, 0:B * OD].rearrange("p (b j) -> p b j", b=B), Ub,
                              ALU.subtract).then_inc(G_("nn_ready"), 1)
            for s in range(3):
                dve.wait_ge(G_("om_done"), s + 1)
                z = acc[0:OD, :].rearrange("p (b d) -> p b d", b=B)
                y = Mg[0:OD]
                if s == 0:
                    dve.scalar_tensor_tensor(out=y, in0=z, scalar=1.0 / 6.0, in1=over_b(Wouth.rearrange(
                        "p (o d) -> p o d", o=1)), op0=ALU.mult, op1=ALU.add).then_inc(G_("om_taken"), 1)
                elif s == 1:
                    dve.tensor_tensor(y, z, over_b(Wout.rearrange("p (o d) -> p o d", o=1)), ALU.add
                                      ).then_inc(G_("om_taken"), 1)
                else:
                    link(dve.tensor_tensor(y, z, over_b(Wout.rearrange("p (o d) -> p o d", o=1)), ALU.add))
            dve.scalar_tensor_tensor(out=Mg[0:OD], in0=Mg[0:OD], scalar=mix[0:OD, :], in1=over_b(idb[0:OD]),
                                     op0=ALU.mult, op1=ALU.add).then_inc(G_("mg_ready"), 1)

            for n, blocks in RMS_GROUPS:
                if n == RMS_GROUPS[-1][0]:
                    dve.wait_ge(G_("x1_ready"), 1)
                    layer_norm(1, 0)
                tiles = blocks * TPK
                dve.wait_ge(G_("a2_sq"), n + blocks)
                link(dve.tensor_scalar(ve[:, 0:tiles], ssq[:, n * TPK:n * TPK + tiles], 1.0 / D, RMS_EPS,
                                       ALU.mult, ALU.add))
                ln_rsqrt(tiles)
                for k in range(blocks):
                    if n + k >= 2:
                        dve.wait_ge(G_("x1_ready"), n + k - 1)
                    for i in range(TPK):
                        c = k * TPK + i
                        ins = dve.scalar_tensor_tensor(out=tA[:, k % 2, i * D:(i + 1) * D],
                                                       in0=bank_a2(n + k)[:, i * D:(i + 1) * D],
                                                       scalar=rs[:, c:c + 1], in1=nwb[:], op0=ALU.mult, op1=ALU.mult)
                    ins.then_inc(G_("t_ready"), 1)

            def add_expert(f, n, e):
                N = NBLK * f + n
                dve.wait_ge(G_("y_done"), E * N + e + 1)
                if not (f == 0 and n_is(n, 0) and e == 0):
                    dve.wait_ge(G_("comb_done"), E * N + e)
                for i in range(TPK):
                    xt = x[:, ds(n * BLK + i * D, D)]
                    ins = dve.scalar_tensor_tensor(out=xt, in0=big[:, 2 + e % 2, i * D:(i + 1) * D],
                                                   scalar=wexp[:, i * E + e:i * E + e + 1], in1=xt,
                                                   op0=ALU.mult, op1=ALU.add)
                ins.then_inc(G_("comb_done"), 1)

            def top_two(N):
                dve.wait_ge(G_("lg_done"), N + 1)
                dve.tensor_copy(lg[:], s1[:, 1, 0:TPK * E].rearrange("p (t e) -> p t e", e=E)
                                ).then_inc(G_("lg_taken"), 1)
                dve.wait_ge(G_("lg_taken"), N + 1)
                dve.memset(pad[:], 0.0)
                for i in range(TPK):
                    ins = dve.max(m8[:, i, :], lg[:, i, :])
                link(ins)
                dve.tensor_tensor(dd[:], m8[:, :, 1], m8[:, :, 0], ALU.subtract).then_inc(G_("d_ready"), 1)
                for i in range(TPK):
                    ins = dve.max_index(ix[:, i, :], m8[:, i, :], lg[:, i, :])
                link(ins)
                link(dve.tensor_copy(ixf[:], ix[:, :, 0:2]))

            def expert_weights(N):
                dve.wait_ge(G_("ed_ready"), N + 1)
                link(dve.tensor_scalar(eds[:], ed[:], 1.0, None, ALU.add))
                link(dve.reciprocal(pr[:, 0, :], eds[:]))
                link(dve.tensor_tensor(pr[:, 1, :], ed[:], pr[:, 0, :], ALU.mult))
                io = iota[:, 0:E].rearrange("p (o e) -> p o e", o=1).broadcast_to([P, TPK, E])
                for s, w in enumerate((wa, wb)):
                    ins = dve.tensor_tensor(w[:], io, ixf[:, :, s:s + 1].broadcast_to([P, TPK, E]), ALU.is_equal)
                link(ins)
                for s, w in enumerate((wa, wb)):
                    ins = dve.tensor_tensor(w[:], w[:], pr[:, s, :].rearrange("p (t o) -> p t o", o=1)
                                            .broadcast_to([P, TPK, E]), ALU.mult)
                link(ins)
                link(dve.tensor_tensor(wexp[:], wa[:].rearrange("p t e -> p (t e)"),
                                       wb[:].rearrange("p t e -> p (t e)"), ALU.add))

            def experts_block(f, n, last, beside=None):
                N = NBLK * f + n
                for e in range(E):
                    dve.wait_ge(G_("relu_done"), CH * E * N + CH * e + 1)
                    if not (f == 0 and n_is(n, 0) and e < 2):
                        dve.wait_ge(G_("y_done"), E * N + e - 1)
                    rl = relu_b[:, (CH * e) % 4, :]
                    dve.tensor_tensor(sq_b[:, 2 * (e % 2), :], rl, rl, ALU.mult).then_inc(G_("sqv_done"), 1)
                    if not last and e == 5:
                        ln_norm(2 * f + 1, n + 1)
                    if e == 0 and not n_is(n, 0):
                        add_expert(f, n - 1, E - 1)
                    if e == 1:
                        top_two(N)
                        expert_weights(N)
                    if e == 2:
                        add_expert(f, n, 0)
                    if e >= 2:
                        add_expert(f, n, e - 1)
                    if not last and e == 3:
                        if f == 0:
                            dve.wait_ge(G_("x1_ready"), NBLK)
                        ln_stats(n + 1)
                    if not last and e == 4:
                        ln_rsqrt()
                    if beside:
                        beside(e)

            def experts(f):
                experts_block(f, 0, False, attention_end if f else None)
                with dve.Fori(1, NBLK - 1) as n:
                    link.enter(n - 1, FFN_CHAIN)
                    experts_block(f, n, False)
                    link.leave(NBLK - 2, FFN_CHAIN)
                experts_block(f, NBLK - 1, True, None if f else attention_start)
                add_expert(f, NBLK - 1, E - 1)

            def attention_start(e):
                if e == 0:
                    layer_norm(2, 0)
                elif e == 2:
                    ln_stats(1)
                elif e == 3:
                    ln_rsqrt()
                    ln_norm(2, 1)
                    split_out(0, 0, 0)
                elif e == 4:
                    split_out(0, 1, 0)
                elif e == 7:
                    split_out(0, 2, 0)

            def attention_end(e):
                if e == 0:
                    normalise(B - 1, 7)
                elif e in (3, 4):
                    add_output(B - 1, e - 3)

            def split_out(count, task, g):
                dve.wait_ge(G_("qkp_taken"), count + task + 1)
                u = task // 2
                if task % 2:
                    dst, mask = Q[:, g, u * BLK:(u + 1) * BLK], nmq
                else:
                    dst, mask = Kst[:], nmk
                    if not (isinstance(count, int) and count + task == 0):
                        dve.wait_ge(G_("km_stored"), count * 32 + u * 64)
                dve.scalar_tensor_tensor(out=dst, in0=tr[:].bitcast(F32), scalar=mask, in1=qf[:, task % 2, :],
                                         op0=ALU.mult, op1=ALU.add).then_inc(G_("qk_split"), 1)

            def maxima(count, kk):
                for i in range(2):
                    t, j = kk // 2, 2 * (kk % 2) + i
                    dve.wait_ge(G_("s1_done"), count + 2 * kk + i + 1)
                    dve.reduce_max(mxp[:, t, j:j + 1], sm[:, i, :], AX.X).then_inc(G_("max_done"), 1)

            def minus_max(count, half):
                dve.wait_ge(G_("max_done"), count + STEPS * (half + 1))
                mh = MX.rearrange("p t (j r) -> p t j r", r=RB)
                mq = mxp[:, TPK * half:TPK * (half + 1)]
                link(dve.tensor_scalar(mh[:, :, :, 24].bitcast(F32R), mq, -1.0, None, ALU.mult))
                dve.scalar_tensor_tensor(out=mh[:, :, :, 25], in0=mq, scalar=-1.0, in1=mh[:, :, :, 24],
                                         op0=ALU.mult, op1=ALU.subtract).then_inc(G_("mx_ready"), 1)

            def shift_queries(count, g, half):
                dve.wait_ge(G_("mxt_done"), count + half + 1)
                qh = Q[:, g, half * BLK:(half + 1) * BLK]
                dve.tensor_tensor(qh, misc[:], qh.bitcast(F32), ALU.add).then_inc(G_("q_shifted"), 1)

            def normalise(b, i):
                g, u = i // 2, i % 2
                dve.wait_ge(G_("ot_done"), 8 * b + i + 1)
                o4 = misc[:].rearrange("p (t j r) -> p t j r", t=TPK, r=RB)
                link(dve.reciprocal(rc[:], o4[:, :, :, DH]))
                dst = ob[:, TPK * u:TPK * (u + 1), HG * DH * g:HG * DH * (g + 1)]
                dve.tensor_tensor(dst.rearrange("p t (j d) -> p t j d", d=DH), o4[:, :, :, 0:DH],
                                  rc[:].rearrange("p t (j o) -> p t j o", o=1).broadcast_to([P, TPK, HG, DH]),
                                  ALU.mult).then_inc(G_("o_normed"), 1)

            experts(0)
            dve.wait_ge(G_("mx_zeroed"), 1)
            split_out(0, 3, 0)
            for kk in range(STEPS):
                maxima(0, kk)
                if kk in (2, 4, 6, 8):
                    split_out(4, kk // 2 - 1, 1)
                if kk == 7:
                    minus_max(0, 0)
                if kk == 10:
                    shift_queries(0, 0, 0)
            minus_max(0, 1)

            def add_output(b, r):
                dve.wait_ge(G_("wo_done"), 2 * b + r + 1)
                dve.wait_ge(G_("x_biased"), 2 * b + r + 1)
                xb = x[:, ds(b * L + r * BLK, BLK)]
                dve.tensor_tensor(xb, misc[:], xb, ALU.add).then_inc(G_("x_added"), 1)

            def attention_batch(b, first, last):
                for k in range(BSTEPS):
                    g, kk = divmod(k, STEPS)
                    more = not (last and g == 3)
                    nxt = 4 * b + g + 1
                    if k == 1 and not first:
                        normalise(b - 1, 7)
                    if kk == 2:
                        shift_queries(2 * (4 * b + g), g, 1)
                    if kk == 3 and g > 0:
                        normalise(b, 2 * g - 1)
                    if k in (9, 10) and not first:
                        add_output(b - 1, k - 9)
                    if kk == 11 and more:
                        shift_queries(2 * nxt, (g + 1) % NG, 0)
                    if kk == 12:
                        normalise(b, 2 * g)
                    if more:
                        maxima(2 * STEPS * nxt, kk)
                    if kk in (4, 5, 6, 7) and not (last and g >= 2):
                        split_out(4 * (4 * b + g + 2), kk - 4, (g + 2) % NG)
                    if kk == 8 and more:
                        minus_max(2 * STEPS * nxt, 0)
                    if kk == 15 and more:
                        minus_max(2 * STEPS * nxt, 1)
                    if not last and g in (0, 1):
                        n = 2 * b + 2 + g
                        if kk == 8:
                            ln_stats(n)
                        if kk == 10:
                            ln_rsqrt()
                        if kk == 12:
                            ln_norm(2, n)
                    if last and g == 3 and kk == 4:
                        layer_norm(3, 0)

            attention_batch(0, True, False)
            with dve.Fori(1, B - 1) as b:
                link.enter(b - 1, ATT_CHAIN)
                attention_batch(b, False, False)
                link.leave(B - 2, ATT_CHAIN)
            attention_batch(B - 1, False, True)
            experts(1)

        @block.tensor
        def _(pe):
            def ln_transpose(kind, n):
                pe.wait_ge(G_("h_ready"), ln_count(kind, n))
                for i in range(TPK):
                    ins = pe.transpose(misc[:, i * P:(i + 1) * P], hb[:, i, :], ident)
                ins.then_inc(G_("lnt_done"), 1)

            pe.wait_ge(G_("cst_loaded"), 16)
            for n in range(NBLK):
                if n >= 2:
                    pe.wait_ge(G_("ht_ready"), n - 1)
                pe.wait_ge(G_("h_ready"), n + 1)
                for i in range(TPK):
                    ins = pe.transpose(bank_a1(n)[:, i * P:(i + 1) * P], hbA[:, n % LNA, i, :], ident)
                ins.then_inc(G_("lnt_done"), 1)
                if n == LNA - 1:
                    pe.wait_ge(G_("attw_loaded"), 64)
                    pe.wait_ge(G_("vq_loaded"), 13 * 16)
                    pe.matmul(s1[0:1, 1, 256:256 + D], bvc[:], woT[:], start=True, stop=True
                              ).then_inc(G_("cbr_done"), 1)
                    pe.wait_ge(G_("cbr_taken"), 1)
                    pe.wait_ge(G_("fills_done"), 1)
                    pe.matmul(s1[:, 0, 0:D], ones[0:1, :], cbrow, start=True, stop=True).then_inc(G_("cbb_done"), 1)

            pe.wait_ge(G_("hm_ready"), 1)
            pe.matmul(s1[0:VD, 0, 0:B], wpi, hm[:], start=True, stop=True)
            pe.matmul(s1[0:B, 0, 64:128], hm[:], wpi, start=True, stop=True).then_inc(G_("vqp_done"), 1)
            pe.wait_ge(G_("wom_loaded"), 16)

            def omega_params(c):
                if c >= 4:
                    pe.wait_ge(G_("par_taken"), c - 3)
                pe.matmul(big[0:B, c % 4, :], hm[:], w_om[:, c * BLK:(c + 1) * BLK], start=True, stop=True
                          ).then_inc(G_("par_done"), 1)

            for c in range(4):
                omega_params(c)
            pe.wait_ge(G_("cn_ready"), 1)
            pe.transpose(s1[0:VD, 1, 0:VC], coden, ident[0:VC, 0:VC])
            pe.transpose(s1[0:VD, 1, VC:VC + B], v4n[:], ident[0:B, 0:B]).then_inc(G_("cnt_done"), 1)
            omega_params(4)
            omega_params(5)
            pe.wait_ge(G_("cnt_taken"), 1)
            pe.matmul(s1[0:B, 1, 64:64 + VC], vnT[:], cnT[:], start=True, stop=True).then_inc(G_("vsc_done"), 1)
            omega_params(6)
            omega_params(7)
            pe.wait_ge(G_("oh_ready"), 1)
            pe.transpose(s1[0:VC, 1, 128:128 + B], oh[:], ident[0:B, 0:B]).then_inc(G_("oht_done"), 1)
            pe.wait_ge(G_("oht_taken"), 1)
            pe.matmul(s1[0:VD, 1, 160:160 + B], code, ohT[:], start=True, stop=True).then_inc(G_("code_done"), 1)
            pe.wait_ge(G_("vq_ready"), 1)
            for b in range(B):
                ins = pe.matmul(s1[0:1, 0, b * D:(b + 1) * D], vqT[:, b:b + 1], wpo, start=True, stop=True)
            ins.then_inc(G_("crow_done"), 1)
            pe.wait_ge(G_("ub_loaded"), 32 * B)
            pe.wait_ge(G_("ht_ready"), NBLK)
            for b in range(B):
                ins = pe.transpose(misc[0:OD, b * OD:(b + 1) * OD], Ub[:, b, :], ident[0:OD, 0:OD])
            ins.then_inc(G_("ubt_done"), 1)
            pe.wait_ge(G_("nn_ready"), 1)
            for s in range(3):
                if s:
                    pe.wait_ge(G_("om_taken"), s)
                for b in range(B):
                    ins = pe.matmul(acc[0:OD, b * D:(b + 1) * D], Nn[:, b, :], Wout if s == 0 else Mg[0:OD, b, :],
                                    start=True, stop=True)
                ins.then_inc(G_("om_done"), 1)
            pe.wait_ge(G_("crow_ready"), 1)

            pe.wait_ge(G_("mg_ready"), 1)
            for n in range(NBLK):
                if n == NBLK - 1:
                    pe.wait_ge(G_("t_ready"), 4)
                for i in range(TPK):
                    T = n * TPK + i
                    pe.matmul(bank_a2(n)[:, i * D:(i + 1) * D], hTa[:, T * P:(T + 1) * P], Mg[:, n // 2, :],
                              start=True, stop=False)
                    ins = pe.matmul(bank_a2(n)[:, i * D:(i + 1) * D], ones[:], crow[:, n // 2, :],
                                    start=False, stop=True)
                ins.then_inc(G_("a2_done"), 1)
            ln_transpose(1, 0)
            pe.wait_ge(G_("t_ready"), 6)

            def n_is(n, v):
                return isinstance(n, int) and n == v

            def three(dst, wh, wl, hoff, width=BLK):
                hh, hl = hTh[:, ds(hoff, width)], hTl[:, ds(hoff, width)]
                pe.matmul(dst, wh, hh, start=True, stop=False)
                pe.matmul(dst, wl, hh, start=False, stop=False)
                return pe.matmul(dst, wh, hl, start=False, stop=True)

            def expert_out(N, e):
                pe.wait_ge(G_("sqv_done"), E * N + e + 1)
                pe.wait_ge(G_("sqa_done"), E * N + e + 1)
                if not (n_is(N, 0) and e < 2):
                    pe.wait_ge(G_("comb_done"), E * N + e - 1)
                for i in range(TPK):
                    for c in range(CH):
                        ins = pe.matmul(big[:, 2 + e % 2, i * D:(i + 1) * D],
                                        sq_b[:, 2 * (e % 2) + c, i * P:(i + 1) * P], w2s[:, CH * e + c, :],
                                        start=(c == 0), stop=(c == CH - 1))
                ins.then_inc(G_("y_done"), 1)

            def experts_block(f, n, last, beside=None):
                N = NBLK * f + n
                hoff = (n % 4) * BLK
                pe.wait_ge(G_("hlo_ready"), 2 * NBLK * f + n + 1)
                three(s1[0:E, 0, :], rwh[:], rwl[:], hoff).then_inc(G_("router_done"), 1)
                for e in range(E):
                    if e == 1:
                        pe.wait_ge(G_("lgt_stored"), N + 1)
                        if not n_is(N, 0):
                            pe.wait_ge(G_("lg_taken"), N)
                    for c in range(CH):
                        q = CH * e + c
                        if not (n_is(N, 0) and q < 2):
                            pe.wait_ge(G_("relu_done"), CH * E * N + q - 1)
                        w = slice(q * P, (q + 1) * P)
                        three(big[:, q % 2, :], w1h[:, w], w1l[:, w], hoff).then_inc(G_("hid_done"), 1)
                    if e == 0 and not n_is(n, 0):
                        expert_out(N - 1, E - 1)
                    if e == 1:
                        for i in range(TPK):
                            ins = pe.transpose(s1[:, 1, i * E:(i + 1) * E], lgT[:, i * P:(i + 1) * P],
                                               ident[0:E, 0:E])
                        ins.then_inc(G_("lg_done"), 1)
                    if e > 0:
                        expert_out(N, e - 1)
                    if e == 6 and not last:
                        pe.wait_ge(G_("ht_ready"), ln_count(2 * f + 1, n))
                        ln_transpose(2 * f + 1, n + 1)
                    if beside:
                        beside(e)

            def experts(f):
                if f == 0:
                    pe.wait_ge(G_("rw_split"), 2)
                    pe.wait_ge(G_("w1_split"), 2)
                    pe.wait_ge(G_("w2_loaded"), 16)
                experts_block(f, 0, False, attention_end if f else None)
                with pe.Fori(1, NBLK - 1) as n:
                    experts_block(f, n, False)
                experts_block(f, NBLK - 1, True, None if f else attention_start)
                expert_out(NBLK * f + NBLK - 1, E - 1)

            def attention_start(e):
                if e == 0:
                    pe.wait_ge(G_("wqk_split"), 4)
                    ln_transpose(2, 0)
                elif e == 2:
                    pe.wait_ge(G_("hlo_ready"), NBLK + 1)
                    project(0, 0, 0, 0)
                elif e == 3:
                    pe.wait_ge(G_("qkp_taken"), 1)
                    project(0, 1, 0, 0)
                elif e == 4:
                    pe.wait_ge(G_("qkp_taken"), 2)
                    ln_transpose(2, 1)
                elif e == 6:
                    pe.wait_ge(G_("hlo_ready"), NBLK + 2)
                    project(0, 2, 0, 0)
                elif e == 7:
                    pe.wait_ge(G_("qkp_taken"), 3)
                    project(0, 3, 0, 0)

            def attention_end(e):
                if e == 0:
                    turn_output(B - 1, 7)
                elif e == 1:
                    pe.wait_ge(G_("o_normed"), 8 * B)
                    output_transpose(B - 1, 0)
                elif e == 2:
                    pe.wait_ge(G_("obt_stored"), 2 * B - 1)
                    output_transpose(B - 1, 1)
                elif e == 3:
                    output_times_wo(B - 1, 0)
                elif e == 4:
                    pe.wait_ge(G_("x_added"), 2 * B - 1)
                    output_times_wo(B - 1, 1)
                elif e == 5:
                    pe.wait_ge(G_("x_added"), 2 * B)

            def project(count, task, g, b):
                wh, wl = ((wkh, wkl), (wqh, wql))[task % 2]
                three(misc[:], wh[:, g, :], wl[:, g, :], (b % 2) * 2 * BLK + (task // 2) * BLK
                      ).then_inc(G_("qkp_done"), 1)

            def values(r):
                for i in range(TPK):
                    ins = pe.matmul(misc[:, i * P:(i + 1) * P], hf[:, r, i * P:(i + 1) * P], wvT[:],
                                    start=True, stop=True)
                ins.then_inc(G_("v_done"), 1)

            def first_pass(count, g, kk, i):
                t, j = kk // 2, 2 * (kk % 2) + i
                if not (isinstance(count, int) and count == 0 and kk == 0):
                    pe.wait_ge(G_("max_done"), count + 2 * kk + i - 1)
                for th in range(2):
                    ins = pe.matmul(sm[:, i, th * BLK:(th + 1) * BLK], Q[:, g, t * P:(t + 1) * P],
                                    Km[:, g, j, th * BLK:(th + 1) * BLK], start=True, stop=True)
                ins.then_inc(G_("s1_done"), 1)

            def turn_maxima(count, half):
                pe.wait_ge(G_("mx_ready"), count + half + 1)
                for i in range(TPK):
                    ins = pe.transpose(misc[:, i * P:(i + 1) * P], MX[:, i, :], ident)
                ins.then_inc(G_("mxt_done"), 1)

            def turn_output(b, i):
                pe.wait_ge(G_("acc_stored"), 8 * b + i + 1)
                for t in range(TPK):
                    ins = pe.transpose(misc[:, t * P:(t + 1) * P], accS[:, t * P:(t + 1) * P], ident)
                ins.then_inc(G_("ot_done"), 1)

            def group_ready(done, g):
                pe.wait_ge(G_("qk_split"), 4 * done + 4)
                pe.wait_ge(G_("km_stored"), 128 * done + 128)

            experts(0)
            pe.wait_ge(G_("comb_done"), E * NBLK)
            pe.wait_ge(G_("qkp_taken"), 4)
            values(0)
            group_ready(0, 0)
            for kk in range(STEPS):
                if kk == 0:
                    pe.wait_ge(G_("v_stored"), 1)
                    values(1)
                elif kk == 1:
                    pe.wait_ge(G_("v_stored"), 2)
                    project(4, 0, 1, 0)
                elif kk in (3, 5, 7):
                    pe.wait_ge(G_("qkp_taken"), 4 + kk // 2)
                    project(4, kk // 2, 1, 0)
                elif kk == 10:
                    pe.wait_ge(G_("qkp_taken"), 8)
                    turn_maxima(0, 0)
                for i in range(2):
                    first_pass(0, 0, kk, i)
            pe.wait_ge(G_("q_shifted"), 1)

            def output_transpose(b, r):
                for t in range(TPK):
                    ins = pe.transpose(misc[:, t * P:(t + 1) * P], ob[:, TPK * r + t, :], ident)
                ins.then_inc(G_("obt_done"), 1)

            def output_times_wo(b, r):
                if r == 0:
                    pe.wait_ge(G_("obt_stored"), 2 * b + 2)
                for t in range(TPK):
                    c = (TPK * r + t) * P
                    ins = pe.matmul(misc[:, t * P:(t + 1) * P], oT2[:, c:c + P], woT[:], start=True, stop=True)
                ins.then_inc(G_("wo_done"), 1)

            def attention_batch(b, first, last):
                prev = None if first else (G_("o_normed"), 8 * b - 1)
                for k in range(BSTEPS):
                    g, kk = divmod(k, STEPS)
                    Gn = 4 * b + g
                    more = not (last and g == 3)
                    u, t = divmod(kk, TPB)

                    def second_pass(j):
                        banks = 2 if more else HG
                        if not (first and k == 0 and j < 2):
                            free = banks if kk or j > 1 else 2
                            pe.wait_ge(G_("exp_done"), HG * (BSTEPS * b + k) + j - free + 1)
                        pe.matmul(sl[:, j % banks, :], Km[:, g, j, t * P:(t + 1) * P],
                                  Q[:, g, u * BLK:(u + 1) * BLK], start=True, stop=True
                                  ).then_inc(G_("s2_done"), 1)

                    if kk == 0:
                        pe.wait_ge(G_("q_shifted"), 2 * Gn + 1)
                        if more:
                            group_ready(Gn + 1, (g + 1) % NG)
                        else:
                            pe.wait_ge(G_("max_done"), 2 * STEPS * NG * B)
                    if kk == 8:
                        pe.wait_ge(G_("q_shifted"), 2 * Gn + 2)
                    second_pass(0)
                    second_pass(1)
                    if not more:
                        second_pass(2)
                    if k > 0:
                        times_values(b, k - 1, first)
                    elif not first:
                        times_values(b - 1, BSTEPS - 1)
                    if more:
                        second_pass(2)
                    second_pass(3)
                    task = None
                    if kk == 2:
                        task = (turn_maxima, (2 * Gn, 1), "q_shifted", 2 * Gn + 2)
                    if kk == 3 and g > 0:
                        task = (turn_output, (b, 2 * g - 1), "o_normed", 8 * b + 2 * g)
                    if not first and k == 1:
                        task = (turn_output, (b - 1, 7), "o_normed", 8 * b)
                    if not first and k in (3, 8):
                        task = (output_transpose, (b - 1, k // 8), "obt_stored", 2 * b - 1 + k // 8)
                    if not first and k in (9, 10):
                        task = (output_times_wo, (b - 1, k - 9), "x_added", 2 * b + k - 10)
                    if kk in (4, 5, 6, 7) and not (last and g >= 2):
                        if g == 2 and kk == 4:
                            pe.wait_ge(G_("hlo_ready"), NBLK + 2 * b + 4)
                        task = (project, (0, kk - 4, (g + 2) % NG, b + g // 2), "qkp_taken", 4 * (Gn + 2) + kk - 3)
                    if kk in (9, 10) and g == 3 and not last:
                        task = (values, (kk - 9,), "v_stored", 2 * b + 3 + kk - 9)
                    if kk == 11 and more:
                        task = (turn_maxima, (2 * (Gn + 1), 0), "q_shifted", 2 * (Gn + 1) + 1)
                    if last and g == 3 and kk == 8:
                        task = (ln_transpose, (3, 0), "ht_ready", ln_count(3, 0))
                    if kk == 14 and g < 2 and not last:
                        task = (ln_transpose, (2, 2 * b + 2 + g), "ht_ready", ln_count(2, 2 * b + 2 + g))
                    if kk == 12:
                        task = (turn_output, (b, 2 * g), "o_normed", 8 * b + 2 * g + 1)
                    if task:
                        if prev is not None:
                            pe.wait_ge(*prev)
                        task[0](*task[1])
                        prev = (G_(task[2]), task[3])
                    if more:
                        first_pass(2 * STEPS * (Gn + 1), (g + 1) % NG, kk, 0)
                        first_pass(2 * STEPS * (Gn + 1), (g + 1) % NG, kk, 1)

            def times_values(b, k, first=False):
                g, kk = divmod(k, STEPS)
                t = kk % TPB
                pe.wait_ge(G_("exp_done"), HG * (BSTEPS * b + k + 1))
                if kk == 0:
                    pe.wait_ge(G_("vg_ready"), 4 * b + g + 1)
                if t == 0 and not (first and k == 0):
                    pe.wait_ge(G_("acc_stored"), 8 * b + k // 8)
                for j in range(HG):
                    ins = pe.matmul(acc[RB * j:RB * (j + 1), :], Vg[:, g % 2, t, j, :], PB[:, k % 2, j, :],
                                    start=(t == 0), stop=(t == TPB - 1))
                ins.then_inc(G_("pv_done"), 1)

            attention_batch(0, True, False)
            with pe.Fori(1, B - 1) as b:
                attention_batch(b, False, False)
            attention_batch(B - 1, False, True)
            times_values(B - 1, BSTEPS - 1)
            pe.wait_ge(G_("o_normed"), 8 * B - 1)
            experts(1)


def kernel(**inputs):
    import numpy as np
    import concourse.bacc as bacc
    from concourse.bass_utils import run_bass_kernel_spmd

    g = {k: np.asarray(v) for k, v in inputs.items()}
    pa, pb, pf = "L0_attn_a_", "L0_attn_b_", "L0_ffn_"
    r, c = np.triu_indices(OD, k=1)

    wom = np.zeros((D, OD * OD), np.float32)
    wom[:, r * OD + c] = g[pa + "omega_proj_w"].T
    bom = np.zeros((1, OD * OD), np.float32)
    bom[0, r * OD + c] = g[pa + "omega_proj_b"]

    def stacked(w):
        o = np.zeros((D, NG, HG, RB), np.float32)
        t = w.reshape(NG, HG, DH, D).transpose(3, 0, 1, 2)
        for k in range(3):
            o[:, :, :, k * DH:(k + 1) * DH] = t
        return o.reshape(D, NG * P)

    def stacked_bias(v, one):
        o = np.zeros((NG, HG, RB), np.float32)
        for k in range(3):
            o[:, :, k * DH:(k + 1) * DH] = v.reshape(NG, HG, DH)
        o[:, :, 3 * DH:3 * DH + 2] = one
        return o.reshape(NG, P).T

    cst = np.zeros((P, C_END), np.float32)
    cst[:, :P] = np.eye(P)
    rows = np.arange(P) % RB
    cst[:, C_NMQ] = np.where((rows >= 2 * DH) & (rows < 3 * DH), -1.0, 0.0)
    cst[:, C_NMK] = np.where((rows >= DH) & (rows < 2 * DH), -1.0, 0.0)
    cst[:, C_IOTA:C_ONE] = np.arange(VC)
    cst[:, C_ONE] = 1.0

    arrays = {
        "x": g[pa + "x"], "cst": cst, "w_om": wom, "b_om": bom,
        "woutT": g[pa + "omega_out_w"].T, "bout": g[pa + "omega_out_b"].reshape(1, D),
        "wpiT": g[pa + "vq_proj_in_w"].T, "bpi": g[pa + "vq_proj_in_b"].reshape(1, VD),
        "wpoT": g[pa + "vq_proj_out_w"].T, "bpo": g[pa + "vq_proj_out_b"].reshape(1, D),
        "cb": g[pa + "codebook"], "mix": g[pa + "omega_mix"].reshape(1, 1),
        "vqm": g[pa + "vq_mix"].reshape(1, 1), "nw": g[pa + "norm_w"].reshape(1, D),
        "wqs": stacked(g[pb + "Wq"]), "wks": stacked(g[pb + "Wk"]),
        "bqs": stacked_bias(g[pb + "bq"], 0.0), "bks": stacked_bias(g[pb + "bk"], 1.0),
        "wvT": g[pb + "Wv"].reshape(H * DH, D).T, "bv": g[pb + "bv"].reshape(1, H * DH),
        "woT": g[pb + "Wo"].T, "bo": g[pb + "bo"].reshape(1, D),
        "rwT": g[pf + "router_w"].T, "w1": g[pf + "w1"], "w2": g[pf + "w2"],
    }
    nc = bacc.Bacc("TRN2", target_bir_lowering=False, num_devices=1)
    feeds, aps = {}, {}
    for name, v in arrays.items():
        v = np.ascontiguousarray(v)
        feeds[f"in_{name}"] = v
        aps[name] = nc.dram_tensor(f"in_{name}", v.shape, mybir.dt.from_np(v.dtype), kind="ExternalInput").ap()
    res = nc.dram_tensor("out_0", (B, L, D), F32, kind="ExternalOutput").ap()
    hybrid_layer(nc, aps, res)
    done = run_bass_kernel_spmd(nc, [feeds], core_ids=[0])
    return done.results[0]["out_0"]
```
